# Optimizing a Trainium2 kernel written in Bass

```python
import numpy as np
import jax
import jax.numpy as jnp

def _softmax(x, axis=-1):
    return jax.nn.softmax(x, axis=axis)

def _gelu(x):
    return jax.nn.gelu(x, approximate=True)

def _silu(x):
    return jax.nn.silu(x)

def _sigmoid(x):
    return jax.nn.sigmoid(x)

def _layernorm(x, axis=-1, eps=1e-05):
    m = jnp.mean(x, axis=axis, keepdims=True)
    v = jnp.var(x, axis=axis, keepdims=True)
    return (x - m) / jnp.sqrt(v + eps)

def _scatter_add(tgt, idx, src, axis=0):
    return tgt.at[idx].add(src)

def _segment_sum(src, seg, n):
    return jax.ops.segment_sum(src, seg, n)
kernel_name = 'mk_xattn_seq_d2_seqx_r8_7b0e6e'

def setup_inputs(seed: int=0):
    np.random.seed(seed)
    _w = jnp.asarray

    def _rec_inputs():
        import jax
        import jax.numpy as jnp
        _rk = jax.random.key(seed)
        x = -0.0003929 + 0.9999 * jax.random.normal(jax.random.fold_in(_rk, 1), (16, 128, 256), jnp.float32)
        _lenS = 128 - jax.random.randint(jax.random.fold_in(_rk, 7), (16,), 0, max(1, 128 // 4) + 1, jnp.int32)
        _lenS2 = 128 - jax.random.randint(jax.random.fold_in(_rk, 8), (16,), 0, max(1, 128 // 4) + 1, jnp.int32)
        _ctx_2048P = jax.random.normal(jax.random.fold_in(_rk, 11), (16, 16, 256), jnp.float32)
        _ctx_2048c = jax.random.dirichlet(jax.random.fold_in(_rk, 511), 0.3 * jnp.ones((16,), jnp.float32), (16, 128))
        _ctx_2048t = jnp.einsum('bsk,bkd->bsd', _ctx_2048c, _ctx_2048P)
        _ctx_2048t = _ctx_2048t * jax.lax.rsqrt(jnp.mean(jnp.square(_ctx_2048t)) + 1e-12) * 0.953939
        ctx_2048 = 2.81802e-05 + 1.00001 * (_ctx_2048t + 0.3 * jax.random.normal(jax.random.fold_in(_rk, 611), (16, 128, 256), jnp.float32))
        return (x, ctx_2048)
    x, ctx_2048 = _rec_inputs()

    def _L0_xattn_setup():
        import jax, jax.numpy as jnp
        import numpy as np
        B, C1, C2, N = (8, 128, 128, 256)
        D = C2 // 8
        key = jax.random.key(seed)
        ks = jax.random.split(key, 8)
        s1 = 1.0 / np.sqrt(C1)
        s2 = 1.0 / np.sqrt(C2)
        return {'x1': jax.random.normal(ks[0], (B, C1, N), jnp.float32), 'x2': jax.random.normal(ks[1], (B, C2, N), jnp.float32), 'Wq': jax.random.uniform(ks[2], (D, C1), jnp.float32, -s1, s1), 'bq': jax.random.uniform(ks[3], (D,), jnp.float32, -s1, s1), 'Wk': jax.random.uniform(ks[4], (D, C2), jnp.float32, -s2, s2), 'bk': jax.random.uniform(ks[5], (D,), jnp.float32, -s2, s2), 'Wv': jax.random.uniform(ks[6], (C1, C2), jnp.float32, -s2, s2), 'bv': jax.random.uniform(ks[7], (C1,), jnp.float32, -s2, s2)}
    _L0_xattn_all = _L0_xattn_setup()
    _L0_xattn_in = {k: v for k, v in _L0_xattn_all.items() if k in ('Wq', 'bq', 'Wk', 'bk', 'Wv', 'bv')}
    del _L0_xattn_all

    def _L1_xattn_setup():
        import jax, jax.numpy as jnp
        import numpy as np
        B, Q, S1, S2 = (4, 32, 256, 256)
        D, H, K, F = (256, 16, 128, 1024)
        LN_EPS = 1e-05

        def _layer_norm(x, scale, offset):
            mu = jnp.mean(x, axis=-1, keepdims=True)
            var = jnp.var(x, axis=-1, keepdims=True)
            return (x - mu) * jax.lax.rsqrt(var + LN_EPS) * scale + offset

        def _cross_attention(q_in, kv_in, wq, bq, wk, bk, wv, bv, wo, bo, bias_k, bias_v):
            b, q_len, _ = q_in.shape
            t = kv_in.shape[1]
            qh = (q_in @ wq + bq).reshape(b, q_len, H, K)
            kh = (kv_in @ wk + bk).reshape(b, t, H, K)
            vh = (kv_in @ wv + bv).reshape(b, t, H, K)
            kh = jnp.concatenate([kh, jnp.broadcast_to(bias_k, (b, 1, H, K))], axis=1)
            vh = jnp.concatenate([vh, jnp.broadcast_to(bias_v, (b, 1, H, K))], axis=1)
            scale = jnp.sqrt(jnp.asarray(K, q_in.dtype))
            logits = jnp.einsum('bqhk,bthk->bhqt', qh, kh) / scale
            weights = jax.nn.softmax(logits, axis=-1)
            ctx = jnp.einsum('bhqt,bthk->bqhk', weights, vh).reshape(b, q_len, H * K)
            return ctx @ wo + bo

        def _forward(x, xf_1, xf_2, ln1_scale, ln1_offset, wq1, bq1, wk1, bk1, wv1, bv1, wo1, bo1, bias_k1, bias_v1, ln2_scale, ln2_offset, wq2, bq2, wk2, bk2, wv2, bv2, wo2, bo2, bias_k2, bias_v2, ln_mlp_scale, ln_mlp_offset, w_fc1, b_fc1, w_fc2, b_fc2):
            res = x
            h = _layer_norm(x, ln1_scale, ln1_offset)
            x = res + _cross_attention(h, xf_1, wq1, bq1, wk1, bk1, wv1, bv1, wo1, bo1, bias_k1, bias_v1)
            res = x
            h = _layer_norm(x, ln2_scale, ln2_offset)
            x = res + _cross_attention(h, xf_2, wq2, bq2, wk2, bk2, wv2, bv2, wo2, bo2, bias_k2, bias_v2)
            h = _layer_norm(x, ln_mlp_scale, ln_mlp_offset)
            h = jax.nn.gelu(h @ w_fc1 + b_fc1, approximate=False) @ w_fc2 + b_fc2
            return x + h
        key = jax.random.key(seed)
        ks = iter(jax.random.split(key, 64))

        def rn(shape, s=0.02):
            return jax.random.normal(next(ks), shape, jnp.float32) * s
        inp = {'x': rn((B, Q, D), 1.0), 'xf_1': rn((B, S1, D), 1.0), 'xf_2': rn((B, S2, D), 1.0)}
        for i in (1, 2):
            inp[f'ln{i}_scale'] = jnp.ones((D,), jnp.float32)
            inp[f'ln{i}_offset'] = jnp.zeros((D,), jnp.float32)
            inp[f'wq{i}'] = rn((D, H * K))
            inp[f'bq{i}'] = jnp.zeros((H * K,), jnp.float32)
            inp[f'wk{i}'] = rn((D, H * K))
            inp[f'bk{i}'] = jnp.zeros((H * K,), jnp.float32)
            inp[f'wv{i}'] = rn((D, H * K))
            inp[f'bv{i}'] = jnp.zeros((H * K,), jnp.float32)
            inp[f'wo{i}'] = rn((H * K, D))
            inp[f'bo{i}'] = jnp.zeros((D,), jnp.float32)
            inp[f'bias_k{i}'] = rn((1, 1, H, K))
            inp[f'bias_v{i}'] = rn((1, 1, H, K))
        inp['ln_mlp_scale'] = jnp.ones((D,), jnp.float32)
        inp['ln_mlp_offset'] = jnp.zeros((D,), jnp.float32)
        inp['w_fc1'] = rn((D, F))
        inp['b_fc1'] = jnp.zeros((F,), jnp.float32)
        inp['w_fc2'] = rn((F, D))
        inp['b_fc2'] = jnp.zeros((D,), jnp.float32)
        return inp
    _L1_xattn_all = _L1_xattn_setup()
    _L1_xattn_in = {k: v for k, v in _L1_xattn_all.items() if k in ('ln1_scale', 'ln1_offset', 'wq1', 'bq1', 'wk1', 'bk1', 'wv1', 'bv1', 'wo1', 'bo1', 'bias_k1', 'bias_v1', 'ln2_scale', 'ln2_offset', 'wq2', 'bq2', 'wk2', 'bk2', 'wv2', 'bv2', 'wo2', 'bo2', 'bias_k2', 'bias_v2', 'ln_mlp_scale', 'ln_mlp_offset', 'w_fc1', 'b_fc1', 'w_fc2', 'b_fc2')}
    del _L1_xattn_all
    return {'x': x, 'ctx_2048': ctx_2048, 'L0_xattn_Wq': _L0_xattn_in['Wq'], 'L0_xattn_bq': _L0_xattn_in['bq'], 'L0_xattn_Wk': _L0_xattn_in['Wk'], 'L0_xattn_bk': _L0_xattn_in['bk'], 'L0_xattn_Wv': _L0_xattn_in['Wv'], 'L0_xattn_bv': _L0_xattn_in['bv'], 'L1_xattn_ln1_scale': _L1_xattn_in['ln1_scale'], 'L1_xattn_ln1_offset': _L1_xattn_in['ln1_offset'], 'L1_xattn_wq1': _L1_xattn_in['wq1'], 'L1_xattn_bq1': _L1_xattn_in['bq1'], 'L1_xattn_wk1': _L1_xattn_in['wk1'], 'L1_xattn_bk1': _L1_xattn_in['bk1'], 'L1_xattn_wv1': _L1_xattn_in['wv1'], 'L1_xattn_bv1': _L1_xattn_in['bv1'], 'L1_xattn_wo1': _L1_xattn_in['wo1'], 'L1_xattn_bo1': _L1_xattn_in['bo1'], 'L1_xattn_bias_k1': _L1_xattn_in['bias_k1'], 'L1_xattn_bias_v1': _L1_xattn_in['bias_v1'], 'L1_xattn_ln2_scale': _L1_xattn_in['ln2_scale'], 'L1_xattn_ln2_offset': _L1_xattn_in['ln2_offset'], 'L1_xattn_wq2': _L1_xattn_in['wq2'], 'L1_xattn_bq2': _L1_xattn_in['bq2'], 'L1_xattn_wk2': _L1_xattn_in['wk2'], 'L1_xattn_bk2': _L1_xattn_in['bk2'], 'L1_xattn_wv2': _L1_xattn_in['wv2'], 'L1_xattn_bv2': _L1_xattn_in['bv2'], 'L1_xattn_wo2': _L1_xattn_in['wo2'], 'L1_xattn_bo2': _L1_xattn_in['bo2'], 'L1_xattn_bias_k2': _L1_xattn_in['bias_k2'], 'L1_xattn_bias_v2': _L1_xattn_in['bias_v2'], 'L1_xattn_ln_mlp_scale': _L1_xattn_in['ln_mlp_scale'], 'L1_xattn_ln_mlp_offset': _L1_xattn_in['ln_mlp_offset'], 'L1_xattn_w_fc1': _L1_xattn_in['w_fc1'], 'L1_xattn_b_fc1': _L1_xattn_in['b_fc1'], 'L1_xattn_w_fc2': _L1_xattn_in['w_fc2'], 'L1_xattn_b_fc2': _L1_xattn_in['b_fc2']}

def reference(x, ctx_2048, L0_xattn_Wq, L0_xattn_bq, L0_xattn_Wk, L0_xattn_bk, L0_xattn_Wv, L0_xattn_bv, L1_xattn_ln1_scale, L1_xattn_ln1_offset, L1_xattn_wq1, L1_xattn_bq1, L1_xattn_wk1, L1_xattn_bk1, L1_xattn_wv1, L1_xattn_bv1, L1_xattn_wo1, L1_xattn_bo1, L1_xattn_bias_k1, L1_xattn_bias_v1, L1_xattn_ln2_scale, L1_xattn_ln2_offset, L1_xattn_wq2, L1_xattn_bq2, L1_xattn_wk2, L1_xattn_bk2, L1_xattn_wv2, L1_xattn_bv2, L1_xattn_wo2, L1_xattn_bo2, L1_xattn_bias_k2, L1_xattn_bias_v2, L1_xattn_ln_mlp_scale, L1_xattn_ln_mlp_offset, L1_xattn_w_fc1, L1_xattn_b_fc1, L1_xattn_w_fc2, L1_xattn_b_fc2):
    import jax
    import jax.numpy as jnp

    def _L0_xattn_ref(x1, x2, Wq, bq, Wk, bk, Wv, bv):
        import jax, jax.numpy as jnp
        import numpy as np
        B, C1, C2, N = (8, 128, 128, 256)
        D = C2 // 8
        q = jnp.einsum('bcn,dc->bnd', x1, Wq) + bq
        k = jnp.einsum('bcn,dc->bdn', x2, Wk) + bk[:, None]
        v = jnp.einsum('bcn,dc->bdn', x2, Wv) + bv[:, None]
        attn = jax.nn.softmax(jnp.einsum('bnd,bdm->bnm', q, k), axis=2)
        attn_out = jnp.einsum('bcm,bnm->bcn', v, attn)
        return attn_out + x1

    def _L1_xattn_ref(x, xf_1, xf_2, ln1_scale, ln1_offset, wq1, bq1, wk1, bk1, wv1, bv1, wo1, bo1, bias_k1, bias_v1, ln2_scale, ln2_offset, wq2, bq2, wk2, bk2, wv2, bv2, wo2, bo2, bias_k2, bias_v2, ln_mlp_scale, ln_mlp_offset, w_fc1, b_fc1, w_fc2, b_fc2):
        import jax, jax.numpy as jnp
        import numpy as np
        B, Q, S1, S2 = (4, 32, 256, 256)
        D, H, K, F = (256, 16, 128, 1024)
        LN_EPS = 1e-05

        def _layer_norm(x, scale, offset):
            mu = jnp.mean(x, axis=-1, keepdims=True)
            var = jnp.var(x, axis=-1, keepdims=True)
            return (x - mu) * jax.lax.rsqrt(var + LN_EPS) * scale + offset

        def _cross_attention(q_in, kv_in, wq, bq, wk, bk, wv, bv, wo, bo, bias_k, bias_v):
            b, q_len, _ = q_in.shape
            t = kv_in.shape[1]
            qh = (q_in @ wq + bq).reshape(b, q_len, H, K)
            kh = (kv_in @ wk + bk).reshape(b, t, H, K)
            vh = (kv_in @ wv + bv).reshape(b, t, H, K)
            kh = jnp.concatenate([kh, jnp.broadcast_to(bias_k, (b, 1, H, K))], axis=1)
            vh = jnp.concatenate([vh, jnp.broadcast_to(bias_v, (b, 1, H, K))], axis=1)
            scale = jnp.sqrt(jnp.asarray(K, q_in.dtype))
            logits = jnp.einsum('bqhk,bthk->bhqt', qh, kh) / scale
            weights = jax.nn.softmax(logits, axis=-1)
            ctx = jnp.einsum('bhqt,bthk->bqhk', weights, vh).reshape(b, q_len, H * K)
            return ctx @ wo + bo

        def _forward(x, xf_1, xf_2, ln1_scale, ln1_offset, wq1, bq1, wk1, bk1, wv1, bv1, wo1, bo1, bias_k1, bias_v1, ln2_scale, ln2_offset, wq2, bq2, wk2, bk2, wv2, bv2, wo2, bo2, bias_k2, bias_v2, ln_mlp_scale, ln_mlp_offset, w_fc1, b_fc1, w_fc2, b_fc2):
            res = x
            h = _layer_norm(x, ln1_scale, ln1_offset)
            x = res + _cross_attention(h, xf_1, wq1, bq1, wk1, bk1, wv1, bv1, wo1, bo1, bias_k1, bias_v1)
            res = x
            h = _layer_norm(x, ln2_scale, ln2_offset)
            x = res + _cross_attention(h, xf_2, wq2, bq2, wk2, bk2, wv2, bv2, wo2, bo2, bias_k2, bias_v2)
            h = _layer_norm(x, ln_mlp_scale, ln_mlp_offset)
            h = jax.nn.gelu(h @ w_fc1 + b_fc1, approximate=False) @ w_fc2 + b_fc2
            return x + h
        return _forward(x, xf_1, xf_2, ln1_scale, ln1_offset, wq1, bq1, wk1, bk1, wv1, bv1, wo1, bo1, bias_k1, bias_v1, ln2_scale, ln2_offset, wq2, bq2, wk2, bk2, wv2, bv2, wo2, bo2, bias_k2, bias_v2, ln_mlp_scale, ln_mlp_offset, w_fc1, b_fc1, w_fc2, b_fc2)
    x = _L0_xattn_ref(x, ctx_2048, L0_xattn_Wq, L0_xattn_bq, L0_xattn_Wk, L0_xattn_bk, L0_xattn_Wv, L0_xattn_bv)
    x = _L1_xattn_ref(x, ctx_2048, ctx_2048, L1_xattn_ln1_scale, L1_xattn_ln1_offset, L1_xattn_wq1, L1_xattn_bq1, L1_xattn_wk1, L1_xattn_bk1, L1_xattn_wv1, L1_xattn_bv1, L1_xattn_wo1, L1_xattn_bo1, L1_xattn_bias_k1, L1_xattn_bias_v1, L1_xattn_ln2_scale, L1_xattn_ln2_offset, L1_xattn_wq2, L1_xattn_bq2, L1_xattn_wk2, L1_xattn_bk2, L1_xattn_wv2, L1_xattn_bv2, L1_xattn_wo2, L1_xattn_bo2, L1_xattn_bias_k2, L1_xattn_bias_v2, L1_xattn_ln_mlp_scale, L1_xattn_ln_mlp_offset, L1_xattn_w_fc1, L1_xattn_b_fc1, L1_xattn_w_fc2, L1_xattn_b_fc2)
    return x

_drawn_inputs = setup_inputs


def setup_inputs(seed=0):
    import zlib

    import numpy as np

    out = dict(_drawn_inputs(seed))
    spreads = {'L1_xattn_ln1_scale': (1.0, 0.6),
     'L1_xattn_ln1_offset': (0.0, 0.8),
     'L1_xattn_bq1': (0.0, 0.8),
     'L1_xattn_bk1': (0.0, 2.0),
     'L1_xattn_bv1': (0.0, 0.1),
     'L1_xattn_bo1': (0.0, 0.1),
     'L1_xattn_ln2_scale': (1.0, 0.6),
     'L1_xattn_ln2_offset': (0.0, 0.8),
     'L1_xattn_bq2': (0.0, 0.8),
     'L1_xattn_bk2': (0.0, 2.0),
     'L1_xattn_bv2': (0.0, 0.1),
     'L1_xattn_bo2': (0.0, 0.1),
     'L1_xattn_ln_mlp_scale': (1.0, 0.6),
     'L1_xattn_ln_mlp_offset': (0.0, 0.697),
     'L1_xattn_b_fc1': (0.0, 0.1),
     'L1_xattn_b_fc2': (0.0, 0.1)}
    factors = {'L0_xattn_bq': 2.858,
     'L0_xattn_bk': 64.0,
     'L1_xattn_wq1': 8.0,
     'L1_xattn_wk1': 8.0,
     'L1_xattn_bias_k1': 64.0,
     'L1_xattn_bias_v1': 64.0,
     'L1_xattn_wq2': 8.0,
     'L1_xattn_wk2': 8.0,
     'L1_xattn_bias_k2': 64.0,
     'L1_xattn_bias_v2': 64.0}
    for name, (base, spread) in spreads.items():
        noise = np.random.default_rng([zlib.crc32(name.encode()), seed]).standard_normal(out[name].shape)
        drawn = base * np.exp(spread * noise) if base else spread * noise
        out[name] = jnp.asarray(drawn.astype(out[name].dtype))
    for name, factor in factors.items():
        out[name] = (out[name] * factor).astype(out[name].dtype)
    return out
```

```python
import concourse.bass as bass
from concourse import mybir
from contextlib import ExitStack

B, P, D = 16, 128, 256
H, K = 16, 128
F = 1024
D0 = 16
LAYERS = 2
HG, BG = 4, 4
NHG, NBG = H // HG, B // BG
STEPS = NHG * NBG
C = D // P
GC = BG * P
FC = F // P
SETS = LAYERS * NHG + 1
PIECES = 5
WQ, WK, WV = 0, C * HG * K, 2 * C * HG * K
PB = 28
BQ, BK, BIASK, BIASV, LNS, LNO, BF1 = 0, 4, 8, 12, 16, 18, 20
TS = P + 1
SCALE = float(K) ** -0.5
EPS = 1e-5


def xattn(nc, x_in, ctx_in, l0w, l0b, l0bv, w_all, rows_all, prm_all, bo_all, out):
    f32, f32r = mybir.dt.float32, mybir.dt.float32r
    ALU, ACT, AX = mybir.AluOpType, mybir.ActivationFunctionType, mybir.AxisListType

    ctx = ExitStack()
    with ctx:
        def sb(name, shape, dt=f32, where=ctx):
            return where.enter_context(nc.sbuf_tensor(name, shape, dt))

        def sem(name):
            return ctx.enter_context(nc.semaphore(name))

        bank = [ctx.enter_context(nc.psum_tensor(f"bank{i}", [P, 512], f32)) for i in range(8)]
        proj_ps = bank[0:2]
        score_ps = bank[2:5]
        pT_ps, cT_ps, out_ps = bank[5], bank[6], bank[7]

        x = sb("x", [P, B, D])
        ctxT = [sb(f"ctxT_{s}", [P, C, B * P], f32r) for s in ("hi", "lo")]
        W = [sb(f"w_{s}", [P, 2, 3 * C * HG * K], f32r) for s in ("hi", "lo")]
        WO = [sb(f"wo_{s}", [P, HG * D], f32r) for s in ("hi", "lo")]
        ring = sb("w_ring", [P, 2, HG * D])
        bvd = sb("bv_less_bias_v", [P, 2, HG * K])
        prm = sb("params", [P, 2, PB])
        bo = sb("bo_rows", [P, 2, D])
        ident = sb("ident", [P, P])
        neg_half = sb("neg_half", [P, BG])
        eps = sb("eps", [P, BG])
        ones = sb("ones", [P, 1])

        w_loaded = [sem(f"w_loaded{i}") for i in range(2)]
        prm_loaded = [sem(f"prm_loaded{i}") for i in range(2)]
        split_hi = sem("split_hi")
        weights_split = sem("weights_split")
        ident_ready = sem("ident_ready")
        l0w_loaded, in_loaded = sem("l0w_loaded"), [sem(f"in_loaded{i}") for i in range(NBG)]
        l0_qk_done, l0_qk_evac = sem("l0_qk_done"), sem("l0_qk_evac")
        l0_v_done, l0_v_evac = sem("l0_v_done"), sem("l0_v_evac")
        l0_cT_done, l0_cT_hi, l0_cT_lo = sem("l0_cT_done"), sem("l0_cT_hi"), sem("l0_cT_lo")
        l0_s_done, l0_nmax, l0_exp = sem("l0_s_done"), sem("l0_nmax"), sem("l0_exp")
        l0_recip, l0_probs = sem("l0_recip"), sem("l0_probs")
        l0_pT_done, l0_pT_copied = sem("l0_pT_done"), sem("l0_pT_copied")
        l0_av_done, l0_added = sem("l0_av_done"), sem("l0_added")
        q_done, k_done, v_done = sem("q_done"), sem("k_done"), sem("v_done")
        q_evac, k_evac, v_evac = sem("q_evac"), sem("k_evac"), sem("v_evac")
        kcol_ready = sem("kcol_ready")
        scores_done, nmax_ready, exp_done = sem("scores_done"), sem("nmax_ready"), sem("exp_done")
        recip_done, probs_ready = sem("recip_done"), sem("probs_ready")
        pT_done, pT_copied = sem("pT_done"), sem("pT_copied")
        cT_done, cT_biased = sem("cT_done"), sem("cT_biased")
        cT_hi_ready, cT_split = sem("cT_hi_ready"), sem("cT_split")
        out_done = sem("out_done")
        x_added = sem("x_added")
        stats_ready, eps_added, rstd_ready = sem("stats_ready"), sem("eps_added"), sem("rstd_ready")
        xn_ready, x_biased = sem("xn_ready"), sem("x_biased")
        lnT_done, ln_tmp, ln_hi, hT_ready = sem("lnT_done"), sem("ln_tmp"), sem("ln_hi"), sem("hT_ready")
        fc1_done, gelu_done, g_hi, g_split = sem("fc1_done"), sem("gelu_done"), sem("g_hi"), sem("g_split")
        fc2_done, y_ready, stored = sem("fc2_done"), sem("y_ready"), sem("stored")

        def at(layer, per_layer, k):
            return layer * per_layer + k

        def pool_copy(pool, dst, src):
            one = ones[:, :]
            for _ in src.shape[2:]:
                one = one.unsqueeze(2)
            return pool.tensor_tensor(dst, src, one.to_broadcast(list(src.shape)), ALU.mult)

        def passes(pe, out_ap, w, m, first=True, last=True):
            for n, (a, b) in enumerate(((0, 0), (0, 1), (1, 0))):
                mm = pe.matmul(out_ap, w[a], m[b], start=first and n == 0, stop=last and n == 2)
            return mm

        def load_set(sp, layer, hg, s):
            n0 = PIECES * (hg + 1)
            slot = (hg + 1) % 2
            sp.dma_start(prm[:, slot, :], prm_all[s]).then_inc(prm_loaded[slot], 16)
            sp.dma_start(bo[:, slot, :], bo_all[s].partition_broadcast(P)).then_inc(prm_loaded[slot], 16)
            for j in range(PIECES):
                if hg >= 0 or j >= 2:
                    sp.wait_ge(weights_split, at(layer, PIECES * NHG, n0 + j - 1))
                dst = ring[:, (n0 + j) % 2, :]
                if j == 3:
                    src = rows_all[s].partition_broadcast(P)
                else:
                    src = w_all[s, j if j < 3 else 3]
                sp.dma_start(dst, src).then_inc(w_loaded[(n0 + j) % 2], 16)

        def split_piece(pool, layer, hg, j):
            n = PIECES * (hg + 1) + j
            slot = (hg + 1) % 2
            pool.wait_ge(w_loaded[n % 2], at(layer, 16 * PIECES * NHG // 2, 16 * (n // 2 + 1)))
            src = ring[:, n % 2, :]
            if j == 3:
                pool.tensor_tensor(bvd[:, slot, :], src[:, 0:HG * K], src[:, HG * K:2 * HG * K],
                                   ALU.subtract).then_inc(weights_split, 1)
                return
            if j < 3:
                hi, lo = (t[:, slot, j * C * HG * K:(j + 1) * C * HG * K] for t in W)
            else:
                hi, lo = (t[:, :] for t in WO)
            n_hi = 4 * (hg + 1) + (j if j < 3 else 3) + 1
            pool_copy(pool, hi, src).then_inc(split_hi, 1)
            pool.wait_ge(split_hi, at(layer, 4 * NHG, n_hi))
            pool.tensor_tensor(lo, src, hi.bitcast(f32), ALU.subtract).then_inc(weights_split, 1)

        with ExitStack() as l0:
            cin = sb("cin", [P, B, D], where=l0)
            l0w_sb = sb("l0w_sb", [P, 2 * D0 + P], where=l0)
            l0b_sb = sb("l0b_sb", [D0, 2], where=l0)
            l0bv_sb = sb("l0bv_sb", [P, P], where=l0)
            qk = sb("l0_qk", [D0, 2, 2, D], where=l0)
            vT = sb("l0_vT", [P, 3, C, P], where=l0)
            prob = sb("l0_prob", [P, 2, C, D], where=l0)
            pT = sb("l0_pT", [P, C, D], where=l0)
            nmax = sb("l0_nmax_t", [P, 2, C], where=l0)
            rsum = sb("l0_rsum", [P, 2, C], where=l0)
            rinv = sb("l0_rinv", [P, 2, C], where=l0)
            qk_ps, v_ps, s_ps, c_ps, av_ps = bank[0], bank[1], bank[2:4], bank[4], bank[7]

            with nc.Block() as block:
                @block.sync
                def _(sp):
                    sp.dma_start(l0w_sb[:, :], l0w).then_inc(l0w_loaded, 16)
                    sp.dma_start(l0b_sb[:, :], l0b).then_inc(l0w_loaded, 16)
                    sp.dma_start(l0bv_sb[:, :], l0bv.partition_broadcast(P)).then_inc(l0w_loaded, 16)
                    for g in range(NBG):
                        s = slice(g * BG, (g + 1) * BG)
                        sp.dma_start(x[:, s, :], x_in[s].rearrange("b p d -> p b d")).then_inc(in_loaded[g], 16)
                        sp.dma_start(cin[:, s, :], ctx_in[s].rearrange("b p d -> p b d")).then_inc(in_loaded[g], 16)
                    load_set(sp, 0, -1, 0)

                @block.gpsimd
                def _(pool):
                    pool.memset(neg_half[:, :], -0.5)
                    pool.memset(ones[:, :], 1.0)
                    pool.memset(eps[:, :], EPS).then_inc(ident_ready, 1)
                    pool.memset(ident[:, :], 0.0).then_inc(ident_ready, 1)
                    pool.wait_ge(ident_ready, 2)
                    pool.affine_select(out=ident[:, :], in_=ident[:, :], compare_op=ALU.not_equal, fill=1.0,
                                       base=0, pattern=[[-1, P]], channel_multiplier=1).then_inc(ident_ready, 1)
                    for j in range(4):
                        split_piece(pool, 0, -1, j)

                @block.tensor
                def _(pe):
                    def project(b):
                        if b % BG == 0:
                            pe.wait_ge(in_loaded[b // BG], 32)
                        if b >= 1:
                            pe.wait_ge(l0_qk_evac, 2 * b)
                        pe.matmul(qk_ps[0:D0, 0:D], l0w_sb[:, 0:D0], x[:, b, :], start=True, stop=True)
                        pe.matmul(qk_ps[0:D0, D:2 * D], l0w_sb[:, D0:2 * D0], cin[:, b, :],
                                  start=True, stop=True).then_inc(l0_qk_done, 1)
                        if b >= 1:
                            pe.wait_ge(l0_v_evac, b)
                        for m in range(C):
                            mm = pe.matmul(v_ps[:, m * P:(m + 1) * P], cin[:, b, m * P:(m + 1) * P],
                                           l0w_sb[:, 2 * D0:2 * D0 + P], start=True, stop=True)
                        mm.then_inc(l0_v_done, 1)
                        if b >= 1:
                            pe.wait_ge(l0_cT_lo, b)
                        for c in range(C):
                            mm = pe.transpose(c_ps[:, c * P:(c + 1) * P], cin[:, b, c * P:(c + 1) * P], ident[:, :])
                        mm.then_inc(l0_cT_done, 1)

                    def scores(b):
                        pe.wait_ge(l0_qk_evac, 2 * (b + 1))
                        if b >= 2:
                            pe.wait_ge(l0_exp, b - 1)
                        for n in range(C):
                            mm = pe.matmul(s_ps[b % 2][:, n * D:(n + 1) * D], qk[:, b % 2, 0, n * P:(n + 1) * P],
                                           qk[:, b % 2, 1, :], start=True, stop=True)
                        mm.then_inc(l0_s_done, 1)

                    def transposes(b):
                        pe.wait_ge(l0_probs, b + 1)
                        for m in range(C):
                            for n in range(C):
                                mm = pe.transpose(pT_ps[:, m * D + n * P:m * D + (n + 1) * P],
                                                  prob[:, b % 2, n, m * P:(m + 1) * P], ident[:, :])
                        mm.then_inc(l0_pT_done, 1)

                    def values(b):
                        pe.wait_ge(l0_pT_copied, b + 1)
                        pe.wait_ge(l0_v_evac, b + 1)
                        if b >= 1:
                            pe.wait_ge(l0_added, b)
                        for m in range(C):
                            mm = pe.matmul(av_ps[:, 0:D], vT[:, b % 3, m, :], pT[:, m, :],
                                           start=m == 0, stop=m == C - 1)
                        mm.then_inc(l0_av_done, 1)

                    pe.wait_ge(l0w_loaded, 48)
                    pe.wait_ge(ident_ready, 3)
                    for i in range(B + 2):
                        if i < B:
                            project(i)
                        if i >= 2:
                            transposes(i - 2)
                        if 1 <= i <= B:
                            scores(i - 1)
                        if i >= 2:
                            values(i - 2)

                @block.scalar
                def _(act):
                    act.wait_ge(l0w_loaded, 48)
                    for i in range(B + 2):
                        if i < B:
                            act.wait_ge(l0_qk_done, i + 1)
                            for j in range(2):
                                act.activation(qk[:, i % 2, j, :], qk_ps[0:D0, j * D:(j + 1) * D], ACT.Identity,
                                               bias=l0b_sb[:, j:j + 1]).then_inc(l0_qk_evac, 1)
                            act.wait_ge(l0_cT_done, i + 1)
                            act.activation(ctxT[0][:, :, i * P:(i + 1) * P],
                                           c_ps[:, 0:D].rearrange("p (c t) -> p c t", c=C),
                                           ACT.Identity).then_inc(l0_cT_hi, 1)
                        if i >= 2:
                            act.wait_ge(l0_pT_done, i - 1)
                            act.activation(pT[:, :, :], pT_ps[:, :].rearrange("p (m n) -> p m n", m=C),
                                           ACT.Identity).then_inc(l0_pT_copied, 1)
                        if 1 <= i <= B:
                            b = i - 1
                            act.wait_ge(l0_nmax, b + 1)
                            for n in range(C):
                                last = act.activation(prob[:, b % 2, n, :], s_ps[b % 2][:, n * D:(n + 1) * D], ACT.Exp,
                                                      bias=nmax[:, b % 2, n:n + 1],
                                                      accum_out=rsum[:, b % 2, n:n + 1])
                            last.then_inc(l0_exp, 1)

                @block.vector
                def _(dve):
                    dve.wait_ge(l0w_loaded, 48)
                    for i in range(B + 2):
                        if i < B:
                            dve.wait_ge(l0_v_done, i + 1)
                            dve.tensor_tensor(vT[:, i % 3, :, :], v_ps[:, 0:D].rearrange("p (m c) -> p m c", m=C),
                                              l0bv_sb[:, :].unsqueeze(1).to_broadcast([P, C, P]),
                                              ALU.add).then_inc(l0_v_evac, 1)
                            dve.wait_ge(l0_cT_hi, i + 1)
                            dve.tensor_tensor(ctxT[1][:, :, i * P:(i + 1) * P],
                                              c_ps[:, 0:D].rearrange("p (c t) -> p c t", c=C),
                                              ctxT[0][:, :, i * P:(i + 1) * P].bitcast(f32),
                                              ALU.subtract).then_inc(l0_cT_lo, 1)
                        if 1 <= i <= B:
                            b = i - 1
                            dve.wait_ge(l0_s_done, b + 1)
                            dve.tensor_reduce(nmax[:, b % 2, :], s_ps[b % 2][:, :].rearrange("p (n m) -> p n m", n=C),
                                              AX.X, ALU.max, negate=True).then_inc(l0_nmax, 1)
                        if i >= 2:
                            b = i - 2
                            dve.wait_ge(l0_av_done, b + 1)
                            dve.tensor_tensor(x[:, b, :], av_ps[:, 0:D], x[:, b, :],
                                              ALU.add).then_inc(l0_added if b < B - 1 else x_added, 1)
                        if 1 <= i <= B:
                            b = i - 1
                            dve.wait_ge(l0_exp, b + 1)
                            dve.reciprocal(rinv[:, b % 2, :], rsum[:, b % 2, :]).then_inc(l0_recip, 1)
                            dve.wait_ge(l0_recip, b + 1)
                            dve.tensor_tensor(prob[:, b % 2, :, :], prob[:, b % 2, :, :],
                                              rinv[:, b % 2, :].unsqueeze(2).to_broadcast([P, C, D]),
                                              ALU.mult).then_inc(l0_probs, 1)

        hT = [sb(f"hT_{s}", [P, C, B * P], f32r) for s in ("hi", "lo")]
        xn = sb("xn", [P, BG, D])
        st6 = sb("ln_st6", [P, BG, 6])
        mv = sb("ln_mv", [P, BG, 2])
        rstd = sb("ln_rstd", [P, BG])
        ln_t = sb("ln_t", [P, GC])

        def ln_dve_stats(dve, layer, bg):
            dve.wait_ge(x_added, at(layer, NHG * B, 1))
            for i in range(BG):
                dve.bn_stats(st6[:, i, :], x[:, bg * BG + i, :])
            dve.drain()
            for i in range(BG):
                last = dve.bn_aggr(mv[:, i, :], st6[:, i, :])
            last.then_inc(stats_ready, 1)

        def ln_pool_rstd(pool, layer, bg):
            pool.wait_ge(stats_ready, at(layer, NBG, bg + 1))
            pool.tensor_tensor(rstd[:, :], mv[:, :, 1], eps[:, :], ALU.add).then_inc(eps_added, 1)
            pool.wait_ge(eps_added, at(layer, NBG, bg + 1))
            pool.tensor_tensor(rstd[:, :], rstd[:, :], neg_half[:, :], ALU.pow).then_inc(rstd_ready, 1)

        def ln_dve_norm(dve, layer, bg):
            dve.wait_ge(rstd_ready, at(layer, NBG, bg + 1))
            for i in range(BG):
                last = dve.tensor_scalar(xn[:, i, :], x[:, bg * BG + i, :], mv[:, i, 0:1], rstd[:, i:i + 1],
                                         ALU.subtract, ALU.mult)
            last.then_inc(xn_ready, 1)

        def ln_pool_bias(pool, layer, bg, slot_wait):
            pool.wait_ge(xn_ready, at(layer, NBG, bg + 1))
            pool.wait_ge(prm_loaded[0], slot_wait)
            pool.tensor_tensor(x[:, bg * BG:(bg + 1) * BG, :], x[:, bg * BG:(bg + 1) * BG, :],
                               bo[:, 0, :].unsqueeze(1).to_broadcast([P, BG, D]), ALU.add).then_inc(x_biased, 1)

        def ln_pe(pe, layer, bg, banks):
            pe.wait_ge(xn_ready, at(layer, NBG, bg + 1))
            for c in range(C):
                for i in range(BG):
                    mm = pe.transpose(banks[c][:, i * P:(i + 1) * P], xn[:, i, c * P:(c + 1) * P], ident[:, :])
                mm.then_inc(lnT_done, 1)

        def ln_act(act, layer, bg, banks, slot_wait):
            act.wait_ge(prm_loaded[0], slot_wait)
            for c in range(C):
                act.wait_ge(lnT_done, at(layer, C * NBG, C * bg + c + 1))
                act.activation(hT[0][:, c, bg * GC:(bg + 1) * GC], banks[c][:, :], ACT.Identity,
                               bias=prm[:, 0, LNO + c:LNO + c + 1],
                               scale=prm[:, 0, LNS + c:LNS + c + 1]).then_inc(ln_hi, 1)

        def ln_dve_split(dve, layer, bg, banks):
            for c in range(C):
                n = at(layer, C * NBG, C * bg + c + 1)
                if C * bg + c:
                    dve.wait_ge(hT_ready, at(layer, C * NBG, C * bg + c))
                dve.wait_ge(ln_hi, n)
                dve.tensor_scalar(ln_t[:, :], banks[c][:, :], prm[:, 0, LNS + c:LNS + c + 1],
                                  prm[:, 0, LNO + c:LNO + c + 1], ALU.mult, ALU.add).then_inc(ln_tmp, 1)
                dve.wait_ge(ln_tmp, n)
                dve.tensor_tensor(hT[1][:, c, bg * GC:(bg + 1) * GC], ln_t[:, :],
                                  hT[0][:, c, bg * GC:(bg + 1) * GC].bitcast(f32),
                                  ALU.subtract).then_inc(hT_ready, 1)

        with ExitStack() as ly:
            QT = sb("qT", [P, HG, GC], where=ly)
            KT = sb("kT", [P, 2, HG, BG, TS], where=ly)
            V = sb("v", [P, BG, HG * K], where=ly)
            prob = sb("prob", [P, 2, HG, TS], where=ly)
            pT = sb("pT", [P, HG * P], where=ly)
            cT = sb("cT", [P, HG, P], where=ly)
            cTs = [sb(f"cT_{s}", [P, 2, HG * P], f32r, where=ly) for s in ("hi", "lo")]
            nmax = sb("nmax", [P, BG, 2, 2], where=ly)
            rsum = sb("rsum", [P, BG, HG], where=ly)
            rinv = sb("rinv", [P, BG, HG], where=ly)
            NQ = NHG * B

            order = [("k", n) for n in range(HG)] + [("v", n) for n in range(BG)]
            for u in range(STEPS):
                order += [("q", HG * u + n) for n in range(HG)]
                if u + 1 < STEPS:
                    order += [("k", HG * (u + 1) + n) for n in range(HG)] + [("v", BG * (u + 1) + n) for n in range(BG)]
            place = {piece: n for n, piece in enumerate(order)}
            evac = {"q": q_evac, "k": k_evac, "v": v_evac}

            def proj_bank(kind, n):
                return proj_ps[place[kind, n] % 2]

            def s_bank(g):
                return score_ps[g % 3]

            def ln_banks(bg):
                return [s_bank(8 * bg), s_bank(8 * bg + 1)]

            with nc.Block() as block:
                @block.sync
                def _(sp):
                    with sp.Fori(0, LAYERS) as layer:
                        for hg in range(NHG):
                            sp.wait_ge(x_added, at(layer, NQ, NBG * BG * hg + 1))
                            load_set(sp, layer, hg, layer * NHG + hg + 1)

                @block.gpsimd
                def _(pool):
                    def key_column(layer, hg, parity):
                        if hg:
                            pool.wait_ge(scores_done, at(layer, 2 * NQ, 8 * (NBG * hg - 1 + parity)))
                        pool.wait_ge(prm_loaded[hg % 2], at(layer, 64, 32 * (hg // 2 + 1)))
                        pool_copy(pool, KT[:, parity, :, :, P],
                                  prm[:, hg % 2, BIASK:BIASK + HG].unsqueeze(2).to_broadcast([P, HG, BG])
                                         ).then_inc(kcol_ready, 1)

                    with pool.Fori(0, LAYERS) as layer:
                        ln_pool_rstd(pool, layer, 0)
                        ln_pool_bias(pool, layer, 0, at(layer, 64, 32))
                        for hg in range(NHG):
                            key_column(layer, hg, 0)
                            pool.wait_ge(x_added, at(layer, NQ, B * hg + 1))
                            split_piece(pool, layer, hg - 1, 4)
                            key_column(layer, hg, 1)
                            for j in range(4):
                                if hg == 0 and j < NBG - 1:
                                    ln_pool_rstd(pool, layer, j + 1)
                                    ln_pool_bias(pool, layer, j + 1, at(layer, 64, 32))
                                split_piece(pool, layer, hg, j)

                @block.tensor
                def _(pe):
                    def free(layer, kind, n):
                        at_n = place[kind, n]
                        if at_n >= 2:
                            k2, n2 = order[at_n - 2]
                            pe.wait_ge(evac[k2], at(layer, NQ, n2 + 1))

                    def queries(layer, u, h):
                        hg, bg = divmod(u, NBG)
                        n = HG * u + h
                        if h == 0:
                            pe.wait_ge(hT_ready, at(layer, C * NBG, C * min(u + 1, NBG)))
                        if bg == 0 and h == 0:
                            pe.wait_ge(weights_split, at(layer, PIECES * NHG, PIECES * hg + 1))
                        free(layer, "q", n)
                        for c in range(C):
                            w = [t[:, hg % 2, WQ + c * HG * K + h * K:WQ + c * HG * K + (h + 1) * K] for t in W]
                            m = [t[:, c, bg * GC:(bg + 1) * GC] for t in hT]
                            mm = passes(pe, proj_bank("q", n)[:, :], w, m, c == 0, c == C - 1)
                        mm.then_inc(q_done, 1)

                    def keys(layer, u, h):
                        hg, bg = divmod(u, NBG)
                        n = HG * u + h
                        if bg == 0 and h == 0:
                            pe.wait_ge(weights_split, at(layer, PIECES * NHG, PIECES * hg + 2))
                        free(layer, "k", n)
                        for c in range(C):
                            w = [t[:, hg % 2, WK + c * HG * K + h * K:WK + c * HG * K + (h + 1) * K] for t in W]
                            m = [t[:, c, bg * GC:(bg + 1) * GC] for t in ctxT]
                            mm = passes(pe, proj_bank("k", n)[:, :], w, m, c == 0, c == C - 1)
                        mm.then_inc(k_done, 1)

                    def vals(layer, u, i):
                        hg, bg = divmod(u, NBG)
                        n = BG * u + i
                        if bg == 0 and i == 0:
                            pe.wait_ge(weights_split, at(layer, PIECES * NHG, PIECES * hg + 3))
                        free(layer, "v", n)
                        for c in range(C):
                            b = bg * BG + i
                            w = [t[:, c, b * P:(b + 1) * P] for t in ctxT]
                            m = [t[:, hg % 2, WV + c * HG * K:WV + (c + 1) * HG * K] for t in W]
                            mm = passes(pe, proj_bank("v", n)[:, :], w, m, c == 0, c == C - 1)
                        mm.then_inc(v_done, 1)

                    def scores(layer, u, i):
                        hg, bg = divmod(u, NBG)
                        if i == 0:
                            pe.wait_ge(q_evac, at(layer, NQ, HG * (u + 1)))
                            pe.wait_ge(k_evac, at(layer, NQ, HG * (u + 1)))
                            if bg < 2:
                                pe.wait_ge(kcol_ready, at(layer, 2 * NHG, 2 * hg + bg + 1))
                        for half in range(2):
                            g = 8 * u + 2 * i + half
                            if g >= 3:
                                pe.wait_ge(exp_done, at(layer, 2 * NQ, g - 2))
                            for j in range(2):
                                h = 2 * half + j
                                mm = pe.matmul(s_bank(g)[:, j * TS:(j + 1) * TS], QT[:, h, i * P:(i + 1) * P],
                                               KT[:, u % 2, h, i, :], start=True, stop=True)
                            mm.then_inc(scores_done, 1)

                    def transposes(layer, u, i):
                        pe.wait_ge(probs_ready, at(layer, NQ, BG * u + i + 1))
                        for h in range(HG):
                            mm = pe.transpose(pT_ps[:, h * P:(h + 1) * P], prob[:, i % 2, h, 0:P], ident[:, :])
                        mm.then_inc(pT_done, 1)

                    def values(layer, u, i):
                        n = BG * u + i + 1
                        pe.wait_ge(pT_copied, at(layer, NQ, n))
                        pe.wait_ge(v_evac, at(layer, NQ, n))
                        if n >= 2:
                            pe.wait_ge(cT_biased, at(layer, NQ, n - 1))
                        for h in range(HG):
                            mm = pe.matmul(cT_ps[:, h * P:(h + 1) * P], V[:, i, h * K:(h + 1) * K],
                                           pT[:, h * P:(h + 1) * P], start=True, stop=True)
                        mm.then_inc(cT_done, 1)

                    def outputs(layer, u, i):
                        hg, bg = divmod(u, NBG)
                        n = BG * u + i
                        if bg == 0 and i == 0:
                            pe.wait_ge(weights_split, at(layer, PIECES * NHG, PIECES * hg + 5))
                        pe.wait_ge(cT_split, at(layer, NQ, n + 1))
                        pe.wait_ge(x_added, at(layer, NQ, n + 1))
                        for h in range(HG):
                            w = [t[:, i % 2, h * P:(h + 1) * P] for t in cTs]
                            m = [t[:, h * D:(h + 1) * D] for t in WO]
                            mm = passes(pe, out_ps[:, 0:D], w, m, h == 0, h == HG - 1)
                        mm.then_inc(out_done, 1)

                    with pe.Fori(0, LAYERS) as layer:
                        for n in range(HG):
                            keys(layer, 0, n)
                        ln_pe(pe, layer, 0, ln_banks(0))
                        for n in range(BG):
                            vals(layer, 0, n)
                        for u in range(STEPS):
                            def ahead(n):
                                if u + 1 < STEPS:
                                    (keys if n < HG else vals)(layer, u + 1, n % HG)
                            for h in range(HG):
                                queries(layer, u, h)
                            ahead(0)
                            scores(layer, u, 0)
                            ahead(1)
                            scores(layer, u, 1)
                            ahead(2)
                            transposes(layer, u, 0)
                            scores(layer, u, 2)
                            ahead(3)
                            values(layer, u, 0)
                            transposes(layer, u, 1)
                            scores(layer, u, 3)
                            ahead(4)
                            values(layer, u, 1)
                            outputs(layer, u, 0)
                            transposes(layer, u, 2)
                            ahead(5)
                            values(layer, u, 2)
                            outputs(layer, u, 1)
                            transposes(layer, u, 3)
                            if u + 1 < NBG:
                                pe.wait_ge(exp_done, at(layer, 2 * NQ, 8 * u + 7))
                                ln_pe(pe, layer, u + 1, ln_banks(u + 1))
                            ahead(6)
                            values(layer, u, 3)
                            outputs(layer, u, 2)
                            ahead(7)
                            outputs(layer, u, 3)

                @block.scalar
                def _(act):
                    def keys_out(layer, u, h):
                        hg = u // NBG
                        n = HG * u + h
                        if u % NBG == 0 and h == 0:
                            act.wait_ge(prm_loaded[hg % 2], at(layer, 64, 32 * (hg // 2 + 1)))
                        act.wait_ge(k_done, at(layer, NQ, n + 1))
                        act.activation(KT[:, u % 2, h, :, 0:P], proj_bank("k", n)[:, :].rearrange("p (b t) -> p b t", b=BG),
                                       ACT.Identity, bias=prm[:, hg % 2, BK + h:BK + h + 1]).then_inc(k_evac, 1)

                    def exps(layer, u, i):
                        for half in range(2):
                            g = 8 * u + 2 * i + half
                            act.wait_ge(nmax_ready, at(layer, 2 * NQ, g + 1))
                            for j in range(2):
                                h = 2 * half + j
                                last = act.activation(prob[:, i % 2, h, :], s_bank(g)[:, j * TS:(j + 1) * TS], ACT.Exp,
                                                      bias=nmax[:, i, half, j:j + 1], accum_out=rsum[:, i, h:h + 1])
                            last.then_inc(exp_done, 1)

                    def pT_out(layer, u, i):
                        act.wait_ge(pT_done, at(layer, NQ, BG * u + i + 1))
                        act.activation(pT[:, :], pT_ps[:, :], ACT.Identity).then_inc(pT_copied, 1)

                    def cT_hi(layer, u, i):
                        act.wait_ge(cT_biased, at(layer, NQ, BG * u + i + 1))
                        act.activation(cTs[0][:, i % 2, :], cT[:, :, :].rearrange("p h q -> p (h q)"),
                                       ACT.Identity).then_inc(cT_hi_ready, 1)

                    with act.Fori(0, LAYERS) as layer:
                        for h in range(HG):
                            keys_out(layer, 0, h)
                        ln_act(act, layer, 0, ln_banks(0), at(layer, 64, 32))
                        for u in range(STEPS):
                            def ahead(h):
                                if u + 1 < STEPS:
                                    keys_out(layer, u + 1, h)
                            ahead(0)
                            exps(layer, u, 0)
                            ahead(1)
                            exps(layer, u, 1)
                            pT_out(layer, u, 0)
                            ahead(2)
                            exps(layer, u, 2)
                            pT_out(layer, u, 1)
                            cT_hi(layer, u, 0)
                            ahead(3)
                            exps(layer, u, 3)
                            cT_hi(layer, u, 1)
                            pT_out(layer, u, 2)
                            cT_hi(layer, u, 2)
                            pT_out(layer, u, 3)
                            if u + 1 < NBG:
                                ln_act(act, layer, u + 1, ln_banks(u + 1), at(layer, 64, 32))
                            cT_hi(layer, u, 3)

                @block.vector
                def _(dve):
                    def queries_out(layer, u, h):
                        hg = u // NBG
                        n = HG * u + h
                        if u % NBG == 0 and h == 0:
                            dve.wait_ge(prm_loaded[hg % 2], at(layer, 64, 32 * (hg // 2 + 1)))
                        dve.wait_ge(q_done, at(layer, NQ, n + 1))
                        dve.tensor_scalar(QT[:, h, :], proj_bank("q", n)[:, :], prm[:, hg % 2, BQ + h:BQ + h + 1],
                                          SCALE, ALU.add, ALU.mult).then_inc(q_evac, 1)

                    def vals_out(layer, u, i):
                        hg = u // NBG
                        n = BG * u + i
                        if u % NBG == 0 and i == 0:
                            dve.wait_ge(weights_split, at(layer, PIECES * NHG, PIECES * hg + 4))
                        dve.wait_ge(v_done, at(layer, NQ, n + 1))
                        dve.tensor_tensor(V[:, i, :], proj_bank("v", n)[:, :], bvd[:, hg % 2, :],
                                          ALU.add).then_inc(v_evac, 1)

                    def maxima(layer, u, i):
                        for half in range(2):
                            g = 8 * u + 2 * i + half
                            dve.wait_ge(scores_done, at(layer, 2 * NQ, g + 1))
                            dve.tensor_reduce(nmax[:, i, half, :], s_bank(g)[:, 0:2 * TS].rearrange("p (j t) -> p j t", j=2),
                                              AX.X, ALU.max, negate=True).then_inc(nmax_ready, 1)

                    def norm(layer, u, i):
                        n = at(layer, NQ, BG * u + i + 1)
                        dve.wait_ge(exp_done, at(layer, 2 * NQ, 8 * u + 2 * i + 2))
                        dve.reciprocal(rinv[:, i, :], rsum[:, i, :]).then_inc(recip_done, 1)
                        dve.wait_ge(recip_done, n)
                        dve.tensor_tensor(prob[:, i % 2, :, 0:P], prob[:, i % 2, :, 0:P],
                                          rinv[:, i, :].unsqueeze(2).to_broadcast([P, HG, P]),
                                          ALU.mult).then_inc(probs_ready, 1)

                    def cT_bias(layer, u, i):
                        hg = u // NBG
                        if u + i:
                            dve.wait_ge(cT_split, at(layer, NQ, BG * u + i))
                        dve.wait_ge(cT_done, at(layer, NQ, BG * u + i + 1))
                        dve.tensor_tensor(cT[:, :, :], cT_ps[:, :].rearrange("p (h q) -> p h q", h=HG),
                                          prm[:, hg % 2, BIASV:BIASV + HG].unsqueeze(2).to_broadcast([P, HG, P]),
                                          ALU.add).then_inc(cT_biased, 1)

                    def cT_lo(layer, u, i):
                        dve.wait_ge(cT_hi_ready, at(layer, NQ, BG * u + i + 1))
                        dve.tensor_tensor(cTs[1][:, i % 2, :], cT[:, :, :].rearrange("p h q -> p (h q)"),
                                          cTs[0][:, i % 2, :].bitcast(f32), ALU.subtract).then_inc(cT_split, 1)

                    def add_out(layer, u, i):
                        hg, bg = divmod(u, NBG)
                        b = bg * BG + i
                        if hg == 0 and i == 0:
                            dve.wait_ge(x_biased, at(layer, NBG, bg + 1))
                        dve.wait_ge(out_done, at(layer, NQ, BG * u + i + 1))
                        dve.tensor_tensor(x[:, b, :], out_ps[:, 0:D], x[:, b, :], ALU.add).then_inc(x_added, 1)

                    with dve.Fori(0, LAYERS) as layer:
                        ln_dve_stats(dve, layer, 0)
                        ln_dve_norm(dve, layer, 0)
                        ln_dve_split(dve, layer, 0, ln_banks(0))
                        for i in range(BG):
                            vals_out(layer, 0, i)
                        for u in range(STEPS):
                            def ahead(i):
                                if u + 1 < STEPS:
                                    vals_out(layer, u + 1, i)
                            for h in range(HG):
                                queries_out(layer, u, h)
                            if u + 1 < NBG:
                                ln_dve_stats(dve, layer, u + 1)
                            maxima(layer, u, 0)
                            maxima(layer, u, 1)
                            norm(layer, u, 0)
                            if u + 1 < NBG:
                                ln_dve_norm(dve, layer, u + 1)
                            maxima(layer, u, 2)
                            norm(layer, u, 1)
                            cT_bias(layer, u, 0)
                            norm(layer, u, 2)
                            maxima(layer, u, 3)
                            cT_lo(layer, u, 0)
                            ahead(0)
                            cT_bias(layer, u, 1)
                            norm(layer, u, 3)
                            cT_lo(layer, u, 1)
                            add_out(layer, u, 0)
                            ahead(1)
                            cT_bias(layer, u, 2)
                            cT_lo(layer, u, 2)
                            add_out(layer, u, 1)
                            if u + 1 < NBG:
                                ln_dve_split(dve, layer, u + 1, ln_banks(u + 1))
                            ahead(2)
                            cT_bias(layer, u, 3)
                            cT_lo(layer, u, 3)
                            add_out(layer, u, 2)
                            ahead(3)
                            add_out(layer, u, 3)

        with ExitStack() as ml:
            g32 = sb("g32", [P, 2, GC], where=ml)
            gs = [sb(f"g_{s}", [P, 3, GC], f32r, where=ml) for s in ("hi", "lo")]
            ln_bk = [score_ps[0], score_ps[1]]
            acc = [score_ps[2], pT_ps, cT_ps, out_ps]
            L = LAYERS
            prm_count = 32 * (SETS + 1) // 2

            def fc2_w(f):
                if f < FC // 2:
                    return [t[:, 0, WV + f * D:WV + (f + 1) * D] for t in W]
                return [t[:, (f - FC // 2) * D:(f - FC // 2 + 1) * D] for t in WO]

            with nc.Block() as block:
                @block.sync
                def _(sp):
                    for bg in range(NBG):
                        s = slice(bg * BG, (bg + 1) * BG)
                        sp.wait_ge(y_ready, BG * (bg + 1))
                        sp.dma_start(out[s].rearrange("b p d -> p b d"), x[:, s, :]).then_inc(stored, 16)
                    sp.wait_ge(stored, 16 * NBG)

                @block.gpsimd
                def _(pool):
                    ln_pool_rstd(pool, L, 0)
                    pool.wait_ge(x_added, L * H // HG * B + 1)
                    split_piece(pool, L - 1, NHG - 1, 4)
                    for bg in range(NBG):
                        if bg:
                            ln_pool_rstd(pool, L, bg)
                        ln_pool_bias(pool, L, bg, prm_count)

                @block.tensor
                def _(pe):
                    def fc1(bg, f):
                        n = FC * bg + f
                        if n >= 2:
                            pe.wait_ge(gelu_done, n - 1)
                        for c in range(C):
                            w = [t[:, 0, c * F + f * P:c * F + (f + 1) * P] for t in W]
                            m = [t[:, c, bg * GC:(bg + 1) * GC] for t in hT]
                            mm = passes(pe, proj_ps[n % 2][:, :], w, m, c == 0, c == C - 1)
                        mm.then_inc(fc1_done, 1)

                    def fc2(bg, f):
                        n = FC * bg + f
                        pe.wait_ge(g_split, n + 1)
                        for i in range(BG):
                            if f == 0 and bg:
                                pe.wait_ge(y_ready, BG * (bg - 1) + i + 1)
                            w = [t[:, n % 3, i * P:(i + 1) * P] for t in gs]
                            mm = passes(pe, acc[i][:, 0:D], w, fc2_w(f), f == 0, f == FC - 1)
                        if f == FC - 1:
                            mm.then_inc(fc2_done, 1)

                    pe.wait_ge(weights_split, PIECES * SETS)
                    ln_pe(pe, L, 0, ln_bk)
                    for bg in range(NBG):
                        pe.wait_ge(hT_ready, C * NBG * L + C * (bg + 1))
                        for f in range(FC + 2):
                            if f < FC:
                                fc1(bg, f)
                            if f == 4 and bg + 1 < NBG:
                                ln_pe(pe, L, bg + 1, ln_bk)
                            if f >= 2:
                                fc2(bg, f - 2)

                @block.scalar
                def _(act):
                    ln_act(act, L, 0, ln_bk, prm_count)
                    for bg in range(NBG):
                        for f in range(FC):
                            n = FC * bg + f
                            act.wait_ge(fc1_done, n + 1)
                            if n >= 2:
                                act.wait_ge(g_split, n - 1)
                            act.activation(g32[:, n % 2, :], proj_ps[n % 2][:, :], ACT.Gelu,
                                           bias=prm[:, 0, BF1 + f:BF1 + f + 1]).then_inc(gelu_done, 1)
                            if f == 5 and bg + 1 < NBG:
                                ln_act(act, L, bg + 1, ln_bk, prm_count)

                @block.vector
                def _(dve):
                    ln_dve_stats(dve, L, 0)
                    ln_dve_norm(dve, L, 0)
                    ln_dve_split(dve, L, 0, ln_bk)
                    for bg in range(NBG):
                        for f in range(FC):
                            n = FC * bg + f
                            dve.wait_ge(gelu_done, n + 1)
                            dve.tensor_copy(gs[0][:, n % 3, :], g32[:, n % 2, :]).then_inc(g_hi, 1)
                            dve.wait_ge(g_hi, n + 1)
                            dve.tensor_tensor(gs[1][:, n % 3, :], g32[:, n % 2, :], gs[0][:, n % 3, :].bitcast(f32),
                                              ALU.subtract).then_inc(g_split, 1)
                            if bg + 1 < NBG:
                                if f == 1:
                                    ln_dve_stats(dve, L, bg + 1)
                                if f == 3:
                                    ln_dve_norm(dve, L, bg + 1)
                                if f == 6:
                                    ln_dve_split(dve, L, bg + 1, ln_bk)
                        dve.wait_ge(x_biased, NBG * L + bg + 1)
                        dve.wait_ge(fc2_done, bg + 1)
                        for i in range(BG):
                            b = bg * BG + i
                            dve.tensor_tensor(x[:, b, :], acc[i][:, 0:D], x[:, b, :], ALU.add).then_inc(y_ready, 1)


def _layout(inputs):
    import numpy as np

    a = {k: np.asarray(v) for k, v in inputs.items()}
    w = np.zeros((SETS, 4, P, HG * D), np.float32)
    rows = np.zeros((SETS, 2 * HG * K), np.float32)
    prm = np.zeros((SETS, P, PB), np.float32)
    bo = np.zeros((SETS, D), np.float32)

    def by_chunk(m):
        return m.reshape(-1, P, m.shape[1]).transpose(1, 0, 2).reshape(P, -1)

    for layer in range(LAYERS):
        g = {k: a[f"L1_xattn_{k}{layer + 1}"] for k in ("wq", "bq", "wk", "bk", "wv", "bv", "wo", "bo", "bias_k", "bias_v")}
        for hg in range(NHG):
            s = layer * NHG + hg
            cols = slice(hg * HG * K, (hg + 1) * HG * K)
            w[s, 0], w[s, 1], w[s, 2] = (by_chunk(g[k][:, cols]) for k in ("wq", "wk", "wv"))
            w[s, 3] = by_chunk(g["wo"][cols])
            rows[s, 0:HG * K] = g["bv"][cols]
            rows[s, HG * K:] = g["bias_v"].reshape(-1)[cols]
            for n, k in ((BQ, "bq"), (BK, "bk"), (BIASK, "bias_k"), (BIASV, "bias_v")):
                prm[s, :, n:n + HG] = g[k].reshape(-1)[cols].reshape(HG, K).T
            prm[s, :, LNS:LNS + C] = a[f"L1_xattn_ln{layer + 1}_scale"].reshape(C, P).T
            prm[s, :, LNO:LNO + C] = a[f"L1_xattn_ln{layer + 1}_offset"].reshape(C, P).T
            bo[s] = g["bo"]
    s = SETS - 1
    fc1 = a["L1_xattn_w_fc1"].reshape(C, P, F)
    w[s, 0], w[s, 1] = fc1[0], fc1[1]
    fc2 = by_chunk(a["L1_xattn_w_fc2"])
    w[s, 2], w[s, 3] = fc2[:, 0:HG * D], fc2[:, HG * D:]
    prm[s, :, LNS:LNS + C] = a["L1_xattn_ln_mlp_scale"].reshape(C, P).T
    prm[s, :, LNO:LNO + C] = a["L1_xattn_ln_mlp_offset"].reshape(C, P).T
    prm[s, :, BF1:BF1 + FC] = a["L1_xattn_b_fc1"].reshape(FC, P).T
    bo[s] = a["L1_xattn_b_fc2"]
    l0w = np.concatenate([a["L0_xattn_Wq"].T, a["L0_xattn_Wk"].T, a["L0_xattn_Wv"].T], axis=1)
    l0b = np.stack([a["L0_xattn_bq"], a["L0_xattn_bk"]], axis=1)
    return {"x_in": a["x"], "ctx_in": a["ctx_2048"], "l0w": l0w, "l0b": l0b, "l0bv": a["L0_xattn_bv"],
            "w_all": w, "rows_all": rows, "prm_all": prm, "bo_all": bo}


def kernel(**inputs):
    import numpy as _np
    import concourse.bacc as _bacc
    from concourse import mybir as _mybir
    from concourse.bass_utils import run_bass_kernel_spmd as _run

    nc = _bacc.Bacc("TRN2", target_bir_lowering=False, num_devices=1)
    arrays = {k: _np.ascontiguousarray(v) for k, v in _layout(inputs).items()}
    args = [nc.dram_tensor(k, v.shape, _mybir.dt.from_np(v.dtype), kind="ExternalInput").ap() for k, v in arrays.items()]
    out = nc.dram_tensor("out", (B, P, D), _mybir.dt.float32, kind="ExternalOutput").ap()
    xattn(nc, *args, out)
    return _run(nc, [arrays], core_ids=[0]).results[0]["out"]
```

```python
import concourse.bass as bass
from concourse import mybir
from contextlib import ExitStack

B, P, D = 16, 128, 256
H, K = 16, 128
F = 1024
D0 = 16
LAYERS = 2
HG, BG = 4, 4
NHG, NBG = H // HG, B // BG
STEPS = NHG * NBG
C = D // P
GC = BG * P
FC = F // P
SETS = LAYERS * NHG + 1
PIECES = 5
WQ, WK, WV = 0, C * HG * K, 2 * C * HG * K
PB = 16
BQ, BK, BIASK, BIASV, BF1 = 0, 4, 8, 12, 0
LNS, LNO = 0, C
NORMS = LAYERS + 1
L0R = 80
L0B = 2 * L0R + P
L0W = L0B + 3
LOADS = [(0, 1), (1, BG)] + [(g * BG, (g + 1) * BG) for g in range(1, NBG)]
LN_AHEAD = STEPS - 2
TS = P + 1
SCALE = float(K) ** -0.5
EPS = 1e-5


def xattn(nc, x_in, ctx_in, l0w, w_all, rows_all, prm_all, ln_all, bo_all, out):
    f32, f32r = mybir.dt.float32, mybir.dt.float32r
    ALU, ACT, AX = mybir.AluOpType, mybir.ActivationFunctionType, mybir.AxisListType

    ctx = ExitStack()
    with ctx:
        def sb(name, shape, dt=f32, where=ctx):
            return where.enter_context(nc.sbuf_tensor(name, shape, dt))

        def sem(name):
            return ctx.enter_context(nc.semaphore(name))

        bank = [ctx.enter_context(nc.psum_tensor(f"bank{i}", [P, 512], f32)) for i in range(8)]
        proj_ps = bank[0:2]
        score_ps = bank[2:5]
        pT_ps, cT_ps, out_ps = bank[5], bank[6], bank[7]

        x = sb("x", [P, B, D])
        ctxT = [sb(f"ctxT_{s}", [P, C, B * P], f32r) for s in ("hi", "lo")]
        W = [sb(f"w_{s}", [P, 2, 3 * C * HG * K], f32r) for s in ("hi", "lo")]
        WO = [sb(f"wo_{s}", [P, HG * D], f32r) for s in ("hi", "lo")]
        ring = sb("w_ring", [P, 2, HG * D])
        bvd = sb("bv_less_bias_v", [P, 2, HG * K])
        prm = sb("params", [P, 2, PB])
        ln_prm = sb("ln_params", [P, 2 * C])
        bo = sb("bo_row", [P, D])
        ident = sb("ident", [P, P])
        neg_half = sb("neg_half", [P, BG])
        eps = sb("eps", [P, BG])
        ones = sb("ones", [P, 1])

        w_loaded = [sem(f"w_loaded{i}") for i in range(2)]
        prm_loaded = [sem(f"prm_loaded{i}") for i in range(2)]
        ln_loaded = sem("ln_loaded")
        split_hi = sem("split_hi")
        weights_split = sem("weights_split")
        ident_ready = sem("ident_ready")
        l0w_loaded, in_loaded = sem("l0w_loaded"), [sem(f"in_loaded{i}") for i in range(len(LOADS))]
        l0_qk_done, l0_qk_hi, l0_qk_split = sem("l0_qk_done"), sem("l0_qk_hi"), sem("l0_qk_split")
        l0_cT_done, l0_cT_out = sem("l0_cT_done"), sem("l0_cT_out")
        l0_cT_hi, l0_cT_lo = sem("l0_cT_hi"), sem("l0_cT_lo")
        l0_s_done, l0_nmax, l0_exp = sem("l0_s_done"), sem("l0_nmax"), sem("l0_exp")
        l0_recip, l0_probs = sem("l0_recip"), sem("l0_probs")
        l0_pT_done, l0_pT_out = sem("l0_pT_done"), sem("l0_pT_out")
        l0_z_done, l0_z_out, l0_out_done = sem("l0_z_done"), sem("l0_z_out"), sem("l0_out_done")
        q_done, k_done, v_done = sem("q_done"), sem("k_done"), sem("v_done")
        q_evac, k_evac, v_evac = sem("q_evac"), sem("k_evac"), sem("v_evac")
        kcol_ready = sem("kcol_ready")
        scores_done, nmax_ready, exp_done = sem("scores_done"), sem("nmax_ready"), sem("exp_done")
        recip_done, probs_ready = sem("recip_done"), sem("probs_ready")
        pT_done, pT_copied = sem("pT_done"), sem("pT_copied")
        cT_done, cT_biased = sem("cT_done"), sem("cT_biased")
        cT_hi_ready, cT_split = sem("cT_hi_ready"), sem("cT_split")
        out_done = sem("out_done")
        x_added = sem("x_added")
        stats_ready, eps_added, rstd_ready = sem("stats_ready"), sem("eps_added"), sem("rstd_ready")
        xn_ready, x_biased = sem("xn_ready"), sem("x_biased")
        lnT_done, ln_out, ln_hi, hT_ready = sem("lnT_done"), sem("ln_out"), sem("ln_hi"), sem("hT_ready")
        fc1_done, gelu_done, g_hi, g_split = sem("fc1_done"), sem("gelu_done"), sem("g_hi"), sem("g_split")
        fc2_done, y_ready, stored = sem("fc2_done"), sem("y_ready"), sem("stored")

        def at(layer, per_layer, k):
            return layer * per_layer + k

        def added(layer, k):
            return layer * (NHG * B) + B + k

        def pool_copy(pool, dst, src):
            one = ones[:, :]
            for _ in src.shape[2:]:
                one = one.unsqueeze(2)
            return pool.tensor_tensor(dst, src, one.to_broadcast(list(src.shape)), ALU.mult)

        def passes(pe, out_ap, w, m, first=True, last=True):
            for n, (a, b) in enumerate(((0, 0), (0, 1), (1, 0))):
                mm = pe.matmul(out_ap, w[a], m[b], start=first and n == 0, stop=last and n == 2)
            return mm

        def load_set(sp, layer, hg, s):
            n0 = PIECES * (hg + 1)
            slot = (hg + 1) % 2
            sp.dma_start(prm[:, slot, :], prm_all[s]).then_inc(prm_loaded[slot], 16)
            for j in range(PIECES):
                if hg >= 0 or j >= 2:
                    sp.wait_ge(weights_split, at(layer, PIECES * NHG, n0 + j - 1))
                dst = ring[:, (n0 + j) % 2, :]
                if j == 3:
                    src = rows_all[s].partition_broadcast(P)
                else:
                    src = w_all[s, j if j < 3 else 3]
                sp.dma_start(dst, src).then_inc(w_loaded[(n0 + j) % 2], 16)

        def load_norm(sp, norm, of=slice(None)):
            sp.dma_start(ln_prm[:, :], ln_all[of][norm]).then_inc(ln_loaded, 16)
            sp.dma_start(bo[:, :], bo_all[of][norm].partition_broadcast(P)).then_inc(ln_loaded, 16)

        def split_piece(pool, layer, hg, j, hi_part=True, lo_part=True):
            n = PIECES * (hg + 1) + j
            slot = (hg + 1) % 2
            if hi_part:
                pool.wait_ge(w_loaded[n % 2], at(layer, 16 * PIECES * NHG // 2, 16 * (n // 2 + 1)))
            src = ring[:, n % 2, :]
            if j == 3:
                pool.tensor_tensor(bvd[:, slot, :], src[:, 0:HG * K], src[:, HG * K:2 * HG * K],
                                   ALU.subtract).then_inc(weights_split, 1)
                return
            if j < 3:
                hi, lo = (t[:, slot, j * C * HG * K:(j + 1) * C * HG * K] for t in W)
            else:
                hi, lo = (t[:, :] for t in WO)
            n_hi = 4 * (hg + 1) + (j if j < 3 else 3) + 1
            if hi_part:
                pool_copy(pool, hi, src).then_inc(split_hi, 1)
            if lo_part:
                pool.wait_ge(split_hi, at(layer, 4 * NHG, n_hi))
                pool.tensor_tensor(lo, src, hi.bitcast(f32), ALU.subtract).then_inc(weights_split, 1)

        hT = [sb(f"hT_{s}", [P, C, B * P], f32r) for s in ("hi", "lo")]
        xn = sb("xn", [P, BG, D])
        st6 = sb("ln_st6", [P, BG, 6])
        mv = sb("ln_mv", [P, BG, 2])
        rstd = sb("ln_rstd", [P, BG])
        ln_t = sb("ln_t", [P, C, GC])

        def ln_dve_stats(dve, norm, bg):
            dve.wait_ge(x_added, at(norm, NHG * B, BG * (bg + 1)))
            for i in range(BG):
                dve.bn_stats(st6[:, i, :], x[:, bg * BG + i, :])
            dve.drain()
            for i in range(BG):
                last = dve.bn_aggr(mv[:, i, :], st6[:, i, :])
            last.then_inc(stats_ready, 1)

        def ln_pool_rstd(pool, norm, bg):
            pool.wait_ge(stats_ready, at(norm, NBG, bg + 1))
            pool.tensor_tensor(rstd[:, :], mv[:, :, 1], eps[:, :], ALU.add).then_inc(eps_added, 1)
            pool.wait_ge(eps_added, at(norm, NBG, bg + 1))
            pool.tensor_tensor(rstd[:, :], rstd[:, :], neg_half[:, :], ALU.pow).then_inc(rstd_ready, 1)

        def ln_dve_norm(dve, norm, bg):
            dve.wait_ge(rstd_ready, at(norm, NBG, bg + 1))
            for i in range(BG):
                last = dve.tensor_scalar(xn[:, i, :], x[:, bg * BG + i, :], mv[:, i, 0:1], rstd[:, i:i + 1],
                                         ALU.subtract, ALU.mult)
            last.then_inc(xn_ready, 1)

        def ln_pool_bias(pool, norm, bg):
            pool.wait_ge(xn_ready, at(norm, NBG, bg + 1))
            pool.wait_ge(ln_loaded, at(norm, 32, 32))
            pool.tensor_tensor(x[:, bg * BG:(bg + 1) * BG, :], x[:, bg * BG:(bg + 1) * BG, :],
                               bo[:, :].unsqueeze(1).to_broadcast([P, BG, D]), ALU.add).then_inc(x_biased, 1)

        def ln_pe(pe, norm, bg, banks):
            pe.wait_ge(xn_ready, at(norm, NBG, bg + 1))
            for c in range(C):
                for i in range(BG):
                    mm = pe.transpose(banks[c][:, i * P:(i + 1) * P], xn[:, i, c * P:(c + 1) * P], ident[:, :])
                mm.then_inc(lnT_done, 1)

        def ln_act(act, norm, bg, banks):
            act.wait_ge(ln_loaded, at(norm, 32, 32))
            for c in range(C):
                n = C * bg + c
                if n >= C:
                    act.wait_ge(hT_ready, at(norm, C * NBG, n - 1))
                act.wait_ge(lnT_done, at(norm, C * NBG, n + 1))
                act.activation(ln_t[:, c, :], banks[c][:, :], ACT.Identity, bias=ln_prm[:, LNO + c:LNO + c + 1],
                               scale=ln_prm[:, LNS + c:LNS + c + 1]).then_inc(ln_out, 1)

        def ln_pool_hi(pool, norm, bg):
            for c in range(C):
                pool.wait_ge(ln_out, at(norm, C * NBG, C * bg + c + 1))
                pool_copy(pool, hT[0][:, c, bg * GC:(bg + 1) * GC], ln_t[:, c, :]).then_inc(ln_hi, 1)

        def ln_dve_lo(dve, norm, bg):
            for c in range(C):
                dve.wait_ge(ln_hi, at(norm, C * NBG, C * bg + c + 1))
                dve.tensor_tensor(hT[1][:, c, bg * GC:(bg + 1) * GC], ln_t[:, c, :],
                                  hT[0][:, c, bg * GC:(bg + 1) * GC].bitcast(f32),
                                  ALU.subtract).then_inc(hT_ready, 1)

        with ExitStack() as l0:
            cin = sb("cin", [P, 3, BG, D], where=l0)
            l0w_sb = sb("l0w_sb", [P, L0W], where=l0)
            l0b_sb = l0w_sb[:, L0B:L0W]
            exp_first = sb("exp_first", [P, 1], where=l0)
            cT0 = sb("l0_cT", [P, 4, D], where=l0)
            qk = sb("l0_qk", [L0R, 2, 2, D], f32r, where=l0)
            prob = sb("l0_prob", [P, 2, C, D], where=l0)
            pT0 = sb("l0_pT", [P, C * D], where=l0)
            z = sb("l0_z", [P, D], where=l0)
            nmax = sb("l0_nmax_t", [P, 2, C], where=l0)
            rsum = sb("l0_rsum", [P, 2, C], where=l0)
            rinv = sb("l0_rinv", [P, 2, C], where=l0)
            qk_ps, z_ps, s_ps, c_ps, av_ps = [bank[0], bank[6]], bank[1], bank[2:4], bank[4], bank[7]
            ln_bk = qk_ps

            with nc.Block() as block:
                @block.sync
                def _(sp):
                    sp.dma_start(l0w_sb[:, :], l0w).then_inc(l0w_loaded, 16)
                    for n, (b0, b1) in enumerate(LOADS):
                        g, i0, i1 = b0 // BG, b0 % BG, (b1 - 1) % BG + 1
                        if g >= 3:
                            sp.wait_ge(l0_cT_done, BG * (g - 2))
                        for dst, src in ((x[:, b0:b1, :], x_in[b0:b1]), (cin[:, g % 3, i0:i1, :], ctx_in[b0:b1])):
                            sp.dma_start(dst, src.rearrange("b p d -> p b d")).then_inc(in_loaded[n], 16)
                    load_norm(sp, 0)
                    load_set(sp, 0, -1, 0)

                @block.gpsimd
                def _(pool):
                    pool.memset(neg_half[:, :], -0.5)
                    pool.memset(ones[:, :], 1.0)
                    pool.memset(eps[:, :], EPS).then_inc(ident_ready, 1)
                    pool.memset(ident[:, :], 0.0).then_inc(ident_ready, 1)
                    pool.wait_ge(ident_ready, 2)
                    pool.affine_select(out=ident[:, :], in_=ident[:, :], compare_op=ALU.not_equal, fill=1.0,
                                       base=0, pattern=[[-1, P]], channel_multiplier=1).then_inc(ident_ready, 1)
                    halves = {6: (0, 0), 7: (0, 1), 9: (1, 0), 11: (1, 1), 12: (2, 0), 13: (2, 1), 14: (3, 0)}
                    for i in range(1, B + 1):
                        pool.wait_ge(l0_recip, i)
                        b = i - 1
                        pool.tensor_tensor(prob[:, b % 2, :, :], prob[:, b % 2, :, :],
                                           rinv[:, b % 2, :].unsqueeze(2).to_broadcast([P, C, D]),
                                           ALU.mult).then_inc(l0_probs, 1)
                        if i == 8:
                            ln_pool_rstd(pool, 0, 0)
                        if i == 10:
                            ln_pool_bias(pool, 0, 0)
                        if i in halves:
                            j, part = halves[i]
                            split_piece(pool, 0, -1, j, hi_part=part == 0, lo_part=part == 1)
                    ln_pool_hi(pool, 0, 0)

                @block.tensor
                def _(pe):
                    def project(b):
                        g, i = divmod(b, BG)
                        for n, (b0, _) in enumerate(LOADS):
                            if b == b0:
                                pe.wait_ge(in_loaded[n], 32)
                        if b >= 2:
                            pe.wait_ge(l0_qk_split, 2 * (b - 1))
                        pe.matmul(qk_ps[b % 2][0:L0R, 0:D], l0w_sb[:, 0:L0R], x[:, b, :], start=True, stop=True)
                        pe.matmul(qk_ps[b % 2][0:L0R, D:2 * D], l0w_sb[:, L0R:2 * L0R], cin[:, g % 3, i, :],
                                  start=True, stop=True).then_inc(l0_qk_done, 1)
                        if b >= 1:
                            pe.wait_ge(l0_cT_out, b)
                        for c in range(C):
                            mm = pe.transpose(c_ps[:, c * P:(c + 1) * P], cin[:, g % 3, i, c * P:(c + 1) * P], ident[:, :])
                        mm.then_inc(l0_cT_done, 1)

                    def scores(b):
                        pe.wait_ge(l0_qk_split, 2 * (b + 1))
                        if b >= 2:
                            pe.wait_ge(l0_exp, b - 1)
                        for n in range(C):
                            mm = pe.matmul(s_ps[b % 2][:, n * D:(n + 1) * D], qk[:, b % 2, 0, n * P:(n + 1) * P],
                                           qk[:, b % 2, 1, :], start=True, stop=True)
                        mm.then_inc(l0_s_done, 1)

                    def transposes(b):
                        pe.wait_ge(l0_probs, b + 1)
                        if b >= 1:
                            pe.wait_ge(l0_pT_out, b)
                        for m in range(C):
                            for n in range(C):
                                mm = pe.transpose(pT_ps[:, m * D + n * P:m * D + (n + 1) * P],
                                                  prob[:, b % 2, n, m * P:(m + 1) * P], ident[:, :])
                        mm.then_inc(l0_pT_done, 1)

                    def mix(b):
                        pe.wait_ge(l0_pT_out, b + 1)
                        if b >= 1:
                            pe.wait_ge(l0_z_out, b)
                        for m in range(C):
                            mm = pe.matmul(z_ps[:, 0:D], cT0[:, b % 4, m * P:(m + 1) * P], pT0[:, m * D:(m + 1) * D],
                                           start=m == 0, stop=m == C - 1)
                        mm.then_inc(l0_z_done, 1)

                    def values(b):
                        pe.wait_ge(l0_z_out, b + 1)
                        if b >= 1:
                            pe.wait_ge(x_added, b)
                        pe.matmul(av_ps[:, 0:D], l0w_sb[:, 2 * L0R:2 * L0R + P], z[:, :],
                                  start=True, stop=True).then_inc(l0_out_done, 1)

                    pe.wait_ge(l0w_loaded, 16)
                    pe.wait_ge(ident_ready, 3)
                    for i in range(B + 4):
                        if i < B:
                            project(i)
                        if 1 <= i <= B:
                            scores(i - 1)
                        if i >= 4:
                            values(i - 4)
                        if 3 <= i < B + 3:
                            mix(i - 3)
                        if i == B:
                            pe.wait_ge(l0_qk_split, 2 * B)
                            ln_pe(pe, 0, 0, ln_bk)
                        if 2 <= i < B + 2:
                            transposes(i - 2)

                @block.scalar
                def _(act):
                    act.wait_ge(ident_ready, 1)
                    act.activation(exp_first[:, :], ones[:, :], ACT.Exp)
                    act.wait_ge(l0w_loaded, 16)
                    for i in range(B + 3):
                        if i < B:
                            act.wait_ge(l0_qk_done, i + 1)
                            for j in range(2):
                                act.activation(qk[:, i % 2, j, :], qk_ps[i % 2][0:L0R, j * D:(j + 1) * D], ACT.Identity,
                                               bias=l0b_sb[0:L0R, j:j + 1]).then_inc(l0_qk_hi, 1)
                            if i >= 4:
                                act.wait_ge(l0_cT_lo, i - 3)
                            act.wait_ge(l0_cT_done, i + 1)
                            act.activation(cT0[:, i % 4, :], c_ps[:, 0:D], ACT.Identity).then_inc(l0_cT_out, 1)
                            act.wait_ge(l0_cT_out, i + 1)
                            act.activation(ctxT[0][:, :, i * P:(i + 1) * P],
                                           cT0[:, i % 4, :].rearrange("p (c t) -> p c t", c=C),
                                           ACT.Identity).then_inc(l0_cT_hi, 1)
                        if 1 <= i <= B:
                            b = i - 1
                            act.wait_ge(l0_nmax, b + 1)
                            for n in range(C):
                                last = act.activation(prob[:, b % 2, n, :], s_ps[b % 2][:, n * D:(n + 1) * D], ACT.Exp,
                                                      bias=nmax[:, b % 2, n:n + 1],
                                                      accum_out=rsum[:, b % 2, n:n + 1])
                            last.then_inc(l0_exp, 1)
                        if i >= 3:
                            act.wait_ge(l0_z_done, i - 2)
                            act.activation(z[:, :], z_ps[:, 0:D], ACT.Identity).then_inc(l0_z_out, 1)
                        if i == B:
                            ln_act(act, 0, 0, ln_bk)
                        if 2 <= i < B + 2:
                            act.wait_ge(l0_pT_done, i - 1)
                            act.activation(pT0[:, :], pT_ps[:, :], ACT.Identity).then_inc(l0_pT_out, 1)

                @block.vector
                def _(dve):
                    for i in range(B + 4):
                        if 1 <= i <= B:
                            b = i - 1
                            dve.wait_ge(l0_s_done, b + 1)
                            dve.tensor_reduce(nmax[:, b % 2, :], s_ps[b % 2][:, :].rearrange("p (n m) -> p n m", n=C),
                                              AX.X, ALU.max, negate=True).then_inc(l0_nmax, 1)
                        if i < B:
                            dve.wait_ge(l0_qk_hi, 2 * (i + 1))
                            for j in range(2):
                                r = slice(32 * (j + 1), 32 * (j + 1) + D0)
                                dve.scalar_tensor_tensor(qk[r, i % 2, j, :], qk_ps[i % 2][r, j * D:(j + 1) * D],
                                                         l0b_sb[r, j:j + 1], qk[r, i % 2, j, :].bitcast(f32),
                                                         ALU.add, ALU.subtract).then_inc(l0_qk_split, 1)
                        if i >= 4:
                            b = i - 4
                            dve.wait_ge(l0_out_done, b + 1)
                            dve.scalar_tensor_tensor(x[:, b, :], av_ps[:, 0:D], l0b_sb[:, 2:3], x[:, b, :],
                                                     ALU.add, ALU.add).then_inc(x_added, 1)
                        if 1 <= i <= B:
                            b = i - 1
                            dve.wait_ge(l0_exp, b + 1)
                            dve.reciprocal(rinv[:, b % 2, :], rsum[:, b % 2, :]).then_inc(l0_recip, 1)
                        if 1 <= i <= B:
                            b = i - 1
                            dve.wait_ge(l0_cT_hi, b + 1)
                            dve.tensor_tensor(ctxT[1][:, :, b * P:(b + 1) * P],
                                              cT0[:, b % 4, :].rearrange("p (c t) -> p c t", c=C),
                                              ctxT[0][:, :, b * P:(b + 1) * P].bitcast(f32),
                                              ALU.subtract).then_inc(l0_cT_lo, 1)
                        if i == 8:
                            ln_dve_stats(dve, 0, 0)
                        if i == 9:
                            ln_dve_norm(dve, 0, 0)
                        if i == B + 2:
                            ln_dve_lo(dve, 0, 0)

        with ExitStack() as ly:
            QT = sb("qT", [P, HG, GC], where=ly)
            KT = sb("kT", [P, 2, HG, BG, TS], where=ly)
            V = sb("v", [P, BG, HG * K], where=ly)
            prob = sb("prob", [P, 2, HG, TS], where=ly)
            pT = sb("pT", [P, HG * P], where=ly)
            cT = sb("cT", [P, HG, P], where=ly)
            cTs = [sb(f"cT_{s}", [P, 2, HG * P], f32r, where=ly) for s in ("hi", "lo")]
            nmax = sb("nmax", [P, BG, 2, 2], where=ly)
            rsum = sb("rsum", [P, BG, HG], where=ly)
            rinv = sb("rinv", [P, BG, HG], where=ly)
            NQ = NHG * B

            order = [("k", n) for n in range(HG)]
            for u in range(STEPS):
                next_k = [("k", HG * (u + 1) + n) for n in range(HG) if u + 1 < STEPS]
                order += [("q", HG * u + n) for n in range(HG)] + next_k[:2]
                order += [("v", BG * u + n) for n in range(BG)] + next_k[2:]
            place = {piece: n for n, piece in enumerate(order)}
            evac = {"q": q_evac, "k": k_evac, "v": v_evac}

            def proj_bank(kind, n):
                return proj_ps[place[kind, n] % 2]

            def s_bank(g):
                return score_ps[g % 3]

            def ln_in(layer, u):
                banks = [s_bank(8 * (u + 1)), s_bank(8 * (u + 1) + 1)]
                if u + 1 < NBG:
                    return layer, u + 1, banks
                if u == LN_AHEAD:
                    return layer + 1, 0, banks

            def ln_step(u):
                return ln_in(0, u) is not None

            with nc.Block() as block:
                @block.sync
                def _(sp):
                    with sp.Fori(0, LAYERS) as layer:
                        for hg in range(NHG):
                            sp.wait_ge(x_added, added(layer, B * hg))
                            load_set(sp, layer, hg, layer * NHG + hg + 1)
                            if hg == 1:
                                load_norm(sp, layer, slice(1, None))

                @block.gpsimd
                def _(pool):
                    def key_column(layer, hg, parity):
                        if hg:
                            pool.wait_ge(scores_done, at(layer, 2 * NQ, 8 * (NBG * hg - 1 + parity)))
                        pool.wait_ge(prm_loaded[hg % 2], at(layer, 32, 16 * (hg // 2 + 1)))
                        pool_copy(pool, KT[:, parity, :, :, P],
                                  prm[:, hg % 2, BIASK:BIASK + HG].unsqueeze(2).to_broadcast([P, HG, BG])
                                         ).then_inc(kcol_ready, 1)

                    with pool.Fori(0, LAYERS) as layer:
                        for hg in range(NHG):
                            if hg:
                                key_column(layer, hg, 0)
                            pool.wait_ge(x_added, added(layer, B * hg))
                            if hg == 0:
                                key_column(layer, hg, 0)
                            split_piece(pool, layer, hg - 1, 4)
                            key_column(layer, hg, 1)
                            for j in range(4):
                                if hg == 0 and ln_step(j):
                                    ln_pool_rstd(pool, layer, j + 1)
                                    ln_pool_bias(pool, layer, j + 1)
                                    ln_pool_hi(pool, layer, j + 1)
                                split_piece(pool, layer, hg, j)
                        ln_pool_rstd(pool, layer + 1, 0)
                        ln_pool_bias(pool, layer + 1, 0)
                        ln_pool_hi(pool, layer + 1, 0)

                @block.tensor
                def _(pe):
                    def free(layer, kind, n):
                        at_n = place[kind, n]
                        if at_n >= 2:
                            k2, n2 = order[at_n - 2]
                            pe.wait_ge(evac[k2], at(layer, NQ, n2 + 1))

                    def queries(layer, u, h):
                        hg, bg = divmod(u, NBG)
                        n = HG * u + h
                        if h == 0:
                            pe.wait_ge(hT_ready, at(layer, C * NBG, C * min(u + 1, NBG)))
                        if bg == 0 and h == 0:
                            pe.wait_ge(weights_split, at(layer, PIECES * NHG, PIECES * hg + 1))
                        free(layer, "q", n)
                        for c in range(C):
                            w = [t[:, hg % 2, WQ + c * HG * K + h * K:WQ + c * HG * K + (h + 1) * K] for t in W]
                            m = [t[:, c, bg * GC:(bg + 1) * GC] for t in hT]
                            mm = passes(pe, proj_bank("q", n)[:, :], w, m, c == 0, c == C - 1)
                        mm.then_inc(q_done, 1)

                    def keys(layer, u, h):
                        hg, bg = divmod(u, NBG)
                        n = HG * u + h
                        if bg == 0 and h == 0:
                            pe.wait_ge(weights_split, at(layer, PIECES * NHG, PIECES * hg + 2))
                        free(layer, "k", n)
                        for c in range(C):
                            w = [t[:, hg % 2, WK + c * HG * K + h * K:WK + c * HG * K + (h + 1) * K] for t in W]
                            m = [t[:, c, bg * GC:(bg + 1) * GC] for t in ctxT]
                            mm = passes(pe, proj_bank("k", n)[:, :], w, m, c == 0, c == C - 1)
                        mm.then_inc(k_done, 1)

                    def vals(layer, u, i):
                        hg, bg = divmod(u, NBG)
                        n = BG * u + i
                        if bg == 0 and i == 0:
                            pe.wait_ge(weights_split, at(layer, PIECES * NHG, PIECES * hg + 3))
                        free(layer, "v", n)
                        for c in range(C):
                            b = bg * BG + i
                            w = [t[:, c, b * P:(b + 1) * P] for t in ctxT]
                            m = [t[:, hg % 2, WV + c * HG * K:WV + (c + 1) * HG * K] for t in W]
                            mm = passes(pe, proj_bank("v", n)[:, :], w, m, c == 0, c == C - 1)
                        mm.then_inc(v_done, 1)

                    def scores(layer, u, i):
                        hg, bg = divmod(u, NBG)
                        if i == 0:
                            pe.wait_ge(q_evac, at(layer, NQ, HG * (u + 1)))
                            pe.wait_ge(k_evac, at(layer, NQ, HG * (u + 1)))
                            if bg < 2:
                                pe.wait_ge(kcol_ready, at(layer, 2 * NHG, 2 * hg + bg + 1))
                        for half in range(2):
                            g = 8 * u + 2 * i + half
                            if g >= 3:
                                pe.wait_ge(exp_done, at(layer, 2 * NQ, g - 2))
                            for j in range(2):
                                h = 2 * half + j
                                mm = pe.matmul(s_bank(g)[:, j * TS:(j + 1) * TS], QT[:, h, i * P:(i + 1) * P],
                                               KT[:, u % 2, h, i, :], start=True, stop=True)
                            mm.then_inc(scores_done, 1)

                    def transposes(layer, u, i):
                        pe.wait_ge(probs_ready, at(layer, NQ, BG * u + i + 1))
                        for h in range(HG):
                            mm = pe.transpose(pT_ps[:, h * P:(h + 1) * P], prob[:, i % 2, h, 0:P], ident[:, :])
                        mm.then_inc(pT_done, 1)

                    def values(layer, u, i):
                        n = BG * u + i + 1
                        pe.wait_ge(pT_copied, at(layer, NQ, n))
                        pe.wait_ge(v_evac, at(layer, NQ, n))
                        if n >= 2:
                            pe.wait_ge(cT_biased, at(layer, NQ, n - 1))
                        for h in range(HG):
                            mm = pe.matmul(cT_ps[:, h * P:(h + 1) * P], V[:, i, h * K:(h + 1) * K],
                                           pT[:, h * P:(h + 1) * P], start=True, stop=True)
                        mm.then_inc(cT_done, 1)

                    def outputs(layer, u, i):
                        hg, bg = divmod(u, NBG)
                        n = BG * u + i
                        if bg == 0 and i == 0:
                            pe.wait_ge(weights_split, at(layer, PIECES * NHG, PIECES * hg + 5))
                        pe.wait_ge(cT_split, at(layer, NQ, n + 1))
                        pe.wait_ge(x_added, added(layer, n))
                        for h in range(HG):
                            w = [t[:, i % 2, h * P:(h + 1) * P] for t in cTs]
                            m = [t[:, h * D:(h + 1) * D] for t in WO]
                            mm = passes(pe, out_ps[:, 0:D], w, m, h == 0, h == HG - 1)
                        mm.then_inc(out_done, 1)

                    with pe.Fori(0, LAYERS) as layer:
                        for n in range(HG):
                            keys(layer, 0, n)
                        for u in range(STEPS):
                            def next_keys(h):
                                if u + 1 < STEPS:
                                    keys(layer, u + 1, h)
                            for h in range(HG):
                                queries(layer, u, h)
                            next_keys(0)
                            scores(layer, u, 0)
                            next_keys(1)
                            scores(layer, u, 1)
                            vals(layer, u, 0)
                            scores(layer, u, 2)
                            transposes(layer, u, 0)
                            vals(layer, u, 1)
                            values(layer, u, 0)
                            transposes(layer, u, 1)
                            scores(layer, u, 3)
                            vals(layer, u, 2)
                            values(layer, u, 1)
                            outputs(layer, u, 0)
                            transposes(layer, u, 2)
                            vals(layer, u, 3)
                            values(layer, u, 2)
                            outputs(layer, u, 1)
                            transposes(layer, u, 3)
                            if ln_step(u):
                                pe.wait_ge(exp_done, at(layer, 2 * NQ, 8 * u + 7))
                                ln_pe(pe, *ln_in(layer, u))
                            next_keys(2)
                            values(layer, u, 3)
                            outputs(layer, u, 2)
                            next_keys(3)
                            outputs(layer, u, 3)

                @block.scalar
                def _(act):
                    def keys_out(layer, u, h):
                        hg = u // NBG
                        n = HG * u + h
                        if u % NBG == 0 and h == 0:
                            act.wait_ge(prm_loaded[hg % 2], at(layer, 32, 16 * (hg // 2 + 1)))
                        act.wait_ge(k_done, at(layer, NQ, n + 1))
                        act.activation(KT[:, u % 2, h, :, 0:P], proj_bank("k", n)[:, :].rearrange("p (b t) -> p b t", b=BG),
                                       ACT.Identity, bias=prm[:, hg % 2, BK + h:BK + h + 1]).then_inc(k_evac, 1)

                    def exps(layer, u, i):
                        for half in range(2):
                            g = 8 * u + 2 * i + half
                            act.wait_ge(nmax_ready, at(layer, 2 * NQ, g + 1))
                            for j in range(2):
                                h = 2 * half + j
                                last = act.activation(prob[:, i % 2, h, :], s_bank(g)[:, j * TS:(j + 1) * TS], ACT.Exp,
                                                      bias=nmax[:, i, half, j:j + 1], accum_out=rsum[:, i, h:h + 1])
                            last.then_inc(exp_done, 1)

                    def pT_out(layer, u, i):
                        act.wait_ge(pT_done, at(layer, NQ, BG * u + i + 1))
                        act.activation(pT[:, :], pT_ps[:, :], ACT.Identity).then_inc(pT_copied, 1)

                    def cT_hi(layer, u, i):
                        act.wait_ge(cT_biased, at(layer, NQ, BG * u + i + 1))
                        act.activation(cTs[0][:, i % 2, :], cT[:, :, :].rearrange("p h q -> p (h q)"),
                                       ACT.Identity).then_inc(cT_hi_ready, 1)

                    with act.Fori(0, LAYERS) as layer:
                        for h in range(HG):
                            keys_out(layer, 0, h)
                        for u in range(STEPS):
                            def next_keys(h):
                                if u + 1 < STEPS:
                                    keys_out(layer, u + 1, h)
                            next_keys(0)
                            exps(layer, u, 0)
                            next_keys(1)
                            exps(layer, u, 1)
                            pT_out(layer, u, 0)
                            exps(layer, u, 2)
                            pT_out(layer, u, 1)
                            cT_hi(layer, u, 0)
                            exps(layer, u, 3)
                            cT_hi(layer, u, 1)
                            pT_out(layer, u, 2)
                            cT_hi(layer, u, 2)
                            pT_out(layer, u, 3)
                            if ln_step(u):
                                ln_act(act, *ln_in(layer, u))
                            next_keys(2)
                            cT_hi(layer, u, 3)
                            next_keys(3)

                @block.vector
                def _(dve):
                    def queries_out(layer, u, h):
                        hg = u // NBG
                        n = HG * u + h
                        if u % NBG == 0 and h == 0:
                            dve.wait_ge(prm_loaded[hg % 2], at(layer, 32, 16 * (hg // 2 + 1)))
                        dve.wait_ge(q_done, at(layer, NQ, n + 1))
                        dve.tensor_scalar(QT[:, h, :], proj_bank("q", n)[:, :], prm[:, hg % 2, BQ + h:BQ + h + 1],
                                          SCALE, ALU.add, ALU.mult).then_inc(q_evac, 1)

                    def vals_out(layer, u, i):
                        hg = u // NBG
                        n = BG * u + i
                        if u % NBG == 0 and i == 0:
                            dve.wait_ge(weights_split, at(layer, PIECES * NHG, PIECES * hg + 4))
                        dve.wait_ge(v_done, at(layer, NQ, n + 1))
                        dve.tensor_tensor(V[:, i, :], proj_bank("v", n)[:, :], bvd[:, hg % 2, :],
                                          ALU.add).then_inc(v_evac, 1)

                    def maxima(layer, u, i):
                        for half in range(2):
                            g = 8 * u + 2 * i + half
                            dve.wait_ge(scores_done, at(layer, 2 * NQ, g + 1))
                            dve.tensor_reduce(nmax[:, i, half, :], s_bank(g)[:, 0:2 * TS].rearrange("p (j t) -> p j t", j=2),
                                              AX.X, ALU.max, negate=True).then_inc(nmax_ready, 1)

                    def norm(layer, u, i):
                        n = at(layer, NQ, BG * u + i + 1)
                        dve.wait_ge(exp_done, at(layer, 2 * NQ, 8 * u + 2 * i + 2))
                        dve.reciprocal(rinv[:, i, :], rsum[:, i, :]).then_inc(recip_done, 1)
                        dve.wait_ge(recip_done, n)
                        dve.tensor_tensor(prob[:, i % 2, :, 0:P], prob[:, i % 2, :, 0:P],
                                          rinv[:, i, :].unsqueeze(2).to_broadcast([P, HG, P]),
                                          ALU.mult).then_inc(probs_ready, 1)

                    def cT_bias(layer, u, i):
                        hg = u // NBG
                        if u + i:
                            dve.wait_ge(cT_split, at(layer, NQ, BG * u + i))
                        dve.wait_ge(cT_done, at(layer, NQ, BG * u + i + 1))
                        dve.tensor_tensor(cT[:, :, :], cT_ps[:, :].rearrange("p (h q) -> p h q", h=HG),
                                          prm[:, hg % 2, BIASV:BIASV + HG].unsqueeze(2).to_broadcast([P, HG, P]),
                                          ALU.add).then_inc(cT_biased, 1)

                    def cT_lo(layer, u, i):
                        dve.wait_ge(cT_hi_ready, at(layer, NQ, BG * u + i + 1))
                        dve.tensor_tensor(cTs[1][:, i % 2, :], cT[:, :, :].rearrange("p h q -> p (h q)"),
                                          cTs[0][:, i % 2, :].bitcast(f32), ALU.subtract).then_inc(cT_split, 1)

                    def add_out(layer, u, i):
                        hg, bg = divmod(u, NBG)
                        b = bg * BG + i
                        if hg == 0 and i == 0:
                            dve.wait_ge(x_biased, at(layer, NBG, bg + 1))
                        dve.wait_ge(out_done, at(layer, NQ, BG * u + i + 1))
                        dve.tensor_tensor(x[:, b, :], out_ps[:, 0:D], x[:, b, :], ALU.add).then_inc(x_added, 1)

                    with dve.Fori(0, LAYERS) as layer:
                        for u in range(STEPS):
                            for h in range(HG):
                                queries_out(layer, u, h)
                            if ln_step(u):
                                ln_dve_stats(dve, *ln_in(layer, u)[:2])
                            maxima(layer, u, 0)
                            maxima(layer, u, 1)
                            norm(layer, u, 0)
                            vals_out(layer, u, 0)
                            maxima(layer, u, 2)
                            norm(layer, u, 1)
                            vals_out(layer, u, 1)
                            cT_bias(layer, u, 0)
                            norm(layer, u, 2)
                            maxima(layer, u, 3)
                            cT_lo(layer, u, 0)
                            vals_out(layer, u, 2)
                            cT_bias(layer, u, 1)
                            norm(layer, u, 3)
                            cT_lo(layer, u, 1)
                            add_out(layer, u, 0)
                            if ln_step(u):
                                ln_dve_norm(dve, *ln_in(layer, u)[:2])
                            vals_out(layer, u, 3)
                            cT_bias(layer, u, 2)
                            cT_lo(layer, u, 2)
                            add_out(layer, u, 1)
                            cT_bias(layer, u, 3)
                            add_out(layer, u, 2)
                            cT_lo(layer, u, 3)
                            if ln_step(u):
                                ln_dve_lo(dve, *ln_in(layer, u)[:2])
                            add_out(layer, u, 3)

        with ExitStack() as ml:
            g32 = sb("g32", [P, 2, GC], where=ml)
            gelu_first = sb("gelu_first", [P, 1], where=ml)
            gs = [sb(f"g_{s}", [P, 3, GC], f32r, where=ml) for s in ("hi", "lo")]
            ln_bk = [score_ps[0], score_ps[1]]
            acc = [score_ps[2], pT_ps, cT_ps, out_ps]
            L = LAYERS
            SET0 = PIECES * (SETS - 1)

            def fc2_w(f):
                if f < FC // 2:
                    return [t[:, 0, WV + f * D:WV + (f + 1) * D] for t in W]
                return [t[:, (f - FC // 2) * D:(f - FC // 2 + 1) * D] for t in WO]

            with nc.Block() as block:
                @block.sync
                def _(sp):
                    for b in range(B):
                        sp.wait_ge(y_ready, b + 1)
                        sp.dma_start(out[b], x[:, b, :]).then_inc(stored, 16)
                    sp.wait_ge(stored, 16 * B)

                @block.gpsimd
                def _(pool):
                    pool.wait_ge(x_added, added(L, 0))
                    split_piece(pool, L - 1, NHG - 1, 4)
                    for bg in range(1, NBG):
                        ln_pool_rstd(pool, L, bg)
                        ln_pool_bias(pool, L, bg)
                        ln_pool_hi(pool, L, bg)

                @block.tensor
                def _(pe):
                    def fc1(bg, f):
                        n = FC * bg + f
                        if n >= 2:
                            pe.wait_ge(gelu_done, n - 1)
                        for c in range(C):
                            w = [t[:, 0, c * F + f * P:c * F + (f + 1) * P] for t in W]
                            m = [t[:, c, bg * GC:(bg + 1) * GC] for t in hT]
                            mm = passes(pe, proj_ps[n % 2][:, :], w, m, c == 0, c == C - 1)
                        mm.then_inc(fc1_done, 1)

                    def fc2(bg, f):
                        n = FC * bg + f
                        if n == 0:
                            pe.wait_ge(weights_split, SET0 + 3)
                        if n == FC // 2:
                            pe.wait_ge(weights_split, SET0 + 5)
                        pe.wait_ge(g_split, n + 1)
                        for i in range(BG):
                            if f == 0 and bg:
                                pe.wait_ge(y_ready, BG * (bg - 1) + i + 1)
                            w = [t[:, n % 3, i * P:(i + 1) * P] for t in gs]
                            mm = passes(pe, acc[i][:, 0:D], w, fc2_w(f), f == 0, f == FC - 1)
                            if f == FC - 1:
                                mm.then_inc(fc2_done, 1)

                    pe.wait_ge(weights_split, SET0 + 2)
                    for bg in range(NBG):
                        pe.wait_ge(hT_ready, C * NBG * L + C * (bg + 1))
                        for f in range(FC + 2):
                            if f < FC:
                                fc1(bg, f)
                            if f == 4 and bg + 1 < NBG:
                                ln_pe(pe, L, bg + 1, ln_bk)
                            if f >= 2:
                                fc2(bg, f - 2)

                @block.scalar
                def _(act):
                    act.activation(gelu_first[:, :], ones[:, :], ACT.Gelu)
                    act.wait_ge(prm_loaded[0], 16 * (SETS + 1) // 2)
                    for bg in range(NBG):
                        for f in range(FC):
                            n = FC * bg + f
                            act.wait_ge(fc1_done, n + 1)
                            if n >= 2:
                                act.wait_ge(g_split, n - 1)
                            act.activation(g32[:, n % 2, :], proj_ps[n % 2][:, :], ACT.Gelu,
                                           bias=prm[:, 0, BF1 + f:BF1 + f + 1]).then_inc(gelu_done, 1)
                            if f == 4 and bg + 1 < NBG:
                                ln_act(act, L, bg + 1, ln_bk)

                @block.vector
                def _(dve):
                    for bg in range(NBG):
                        for f in range(FC):
                            n = FC * bg + f
                            dve.wait_ge(gelu_done, n + 1)
                            dve.tensor_copy(gs[0][:, n % 3, :], g32[:, n % 2, :]).then_inc(g_hi, 1)
                            dve.wait_ge(g_hi, n + 1)
                            dve.tensor_tensor(gs[1][:, n % 3, :], g32[:, n % 2, :], gs[0][:, n % 3, :].bitcast(f32),
                                              ALU.subtract).then_inc(g_split, 1)
                            if bg + 1 < NBG:
                                if f == 0:
                                    ln_dve_stats(dve, L, bg + 1)
                                if f == 2:
                                    ln_dve_norm(dve, L, bg + 1)
                                if f == 6:
                                    ln_dve_lo(dve, L, bg + 1)
                        dve.wait_ge(x_biased, NBG * L + bg + 1)
                        for i in range(BG):
                            b = bg * BG + i
                            dve.wait_ge(fc2_done, b + 1)
                            dve.tensor_tensor(x[:, b, :], acc[i][:, 0:D], x[:, b, :], ALU.add).then_inc(y_ready, 1)


def _layout(inputs):
    import numpy as np

    a = {k: np.asarray(v) for k, v in inputs.items()}
    w = np.zeros((SETS, 4, P, HG * D), np.float32)
    rows = np.zeros((SETS, 2 * HG * K), np.float32)
    prm = np.zeros((SETS, P, PB), np.float32)
    ln = np.stack([np.concatenate([a[f"L1_xattn_{k}_scale"].reshape(C, P).T, a[f"L1_xattn_{k}_offset"].reshape(C, P).T], axis=1)
                   for k in ("ln1", "ln2", "ln_mlp")])
    bo = np.stack([a["L1_xattn_bo1"], a["L1_xattn_bo2"], a["L1_xattn_b_fc2"]])

    def by_chunk(m):
        return m.reshape(-1, P, m.shape[1]).transpose(1, 0, 2).reshape(P, -1)

    for layer in range(LAYERS):
        g = {k: a[f"L1_xattn_{k}{layer + 1}"] for k in ("wq", "bq", "wk", "bk", "wv", "bv", "wo", "bo", "bias_k", "bias_v")}
        for hg in range(NHG):
            s = layer * NHG + hg
            cols = slice(hg * HG * K, (hg + 1) * HG * K)
            w[s, 0], w[s, 1], w[s, 2] = (by_chunk(g[k][:, cols]) for k in ("wq", "wk", "wv"))
            w[s, 3] = by_chunk(g["wo"][cols])
            rows[s, 0:HG * K] = g["bv"][cols]
            rows[s, HG * K:] = g["bias_v"].reshape(-1)[cols]
            for n, k in ((BQ, "bq"), (BK, "bk"), (BIASK, "bias_k"), (BIASV, "bias_v")):
                prm[s, :, n:n + HG] = g[k].reshape(-1)[cols].reshape(HG, K).T
    s = SETS - 1
    fc1 = a["L1_xattn_w_fc1"].reshape(C, P, F)
    w[s, 0], w[s, 1] = fc1[0], fc1[1]
    fc2 = by_chunk(a["L1_xattn_w_fc2"])
    w[s, 2], w[s, 3] = fc2[:, 0:HG * D], fc2[:, HG * D:]
    prm[s, :, BF1:BF1 + FC] = a["L1_xattn_b_fc1"].reshape(FC, P).T
    l0w = np.zeros((P, L0W), np.float32)
    for n in (0, 32, 64):
        l0w[:, n:n + D0], l0w[:, L0R + n:L0R + n + D0] = a["L0_xattn_Wq"].T, a["L0_xattn_Wk"].T
        l0w[n:n + D0, L0B], l0w[n:n + D0, L0B + 1] = a["L0_xattn_bq"], a["L0_xattn_bk"]
    l0w[:, 2 * L0R:L0B] = a["L0_xattn_Wv"].T
    l0w[:, L0B + 2] = a["L0_xattn_bv"]
    return {"x_in": a["x"], "ctx_in": a["ctx_2048"], "l0w": l0w,
            "w_all": w, "rows_all": rows, "prm_all": prm, "ln_all": ln, "bo_all": bo}


def kernel(**inputs):
    import numpy as _np
    import concourse.bacc as _bacc
    from concourse import mybir as _mybir
    from concourse.bass_utils import run_bass_kernel_spmd as _run

    nc = _bacc.Bacc("TRN2", target_bir_lowering=False, num_devices=1)
    arrays = {k: _np.ascontiguousarray(v) for k, v in _layout(inputs).items()}
    args = [nc.dram_tensor(k, v.shape, _mybir.dt.from_np(v.dtype), kind="ExternalInput").ap() for k, v in arrays.items()]
    out = nc.dram_tensor("out", (B, P, D), _mybir.dt.float32, kind="ExternalOutput").ap()
    xattn(nc, *args, out)
    return _run(nc, [arrays], core_ids=[0]).results[0]["out"]
```
